# Optimizing a Trainium2 kernel written in Bass

```python
import numpy as np
import jax
import jax.numpy as jnp

def _softmax(x, axis=-1):
    return jax.nn.softmax(x, axis=axis)

def _gelu(x):
    return jax.nn.gelu(x, approximate=True)

def _silu(x):
    return jax.nn.silu(x)

def _sigmoid(x):
    return jax.nn.sigmoid(x)

def _layernorm(x, axis=-1, eps=1e-05):
    m = jnp.mean(x, axis=axis, keepdims=True)
    v = jnp.var(x, axis=axis, keepdims=True)
    return (x - m) / jnp.sqrt(v + eps)

def _scatter_add(tgt, idx, src, axis=0):
    return tgt.at[idx].add(src)

def _segment_sum(src, seg, n):
    return jax.ops.segment_sum(src, seg, n)
kernel_name = 'mk_adj_preln_d1_adj_r2_024428'

def setup_inputs(seed: int=0):
    np.random.seed(seed)
    _w = jnp.asarray

    def _rec_inputs():
        import jax
        import jax.numpy as jnp
        _gk = jax.random.key(seed)
        x = -0.0002928 + 1 * jax.random.normal(jax.random.fold_in(_gk, 1), (8, 1024, 256), jnp.float32)
        _a = jax.random.bernoulli(jax.random.fold_in(_gk, 2), 0.015625, (8, 1024, 1024))
        _a = jnp.logical_or(_a, jnp.swapaxes(_a, -1, -2))
        _a = jnp.logical_or(_a, jnp.eye(1024, dtype=bool))
        adj = _a.astype(jnp.int32)
        return (x, adj)
    x, adj = _rec_inputs()

    def _L0_gnn_setup():
        import jax, jax.numpy as jnp
        import numpy as np
        L = 3
        D = 256
        B, N = (8, 512)
        EPS = 1e-05

        def layernorm(x, gamma, beta):
            mu = jnp.mean(x, axis=-1, keepdims=True)
            var = jnp.var(x, axis=-1, keepdims=True)
            return (x - mu) * jax.lax.rsqrt(var + EPS) * gamma + beta
        key = jax.random.key(seed)
        ks = jax.random.split(key, 12)
        s = 1.0 / np.sqrt(D)
        node_features = jax.random.normal(ks[0], (B, N, D), dtype=jnp.float32)
        adjacency_matrix = jax.random.randint(ks[1], (B, N, N), 0, 2, dtype=jnp.int32)
        return {'node_features': node_features, 'adjacency_matrix': adjacency_matrix, 'attn_w': jax.random.normal(ks[2], (L, 2 * D), dtype=jnp.float32) * (1.0 / np.sqrt(2 * D)), 'attn_b': jax.random.normal(ks[3], (L,), dtype=jnp.float32) * 0.01, 'W1': jax.random.normal(ks[4], (L, D, 4 * D), dtype=jnp.float32) * s, 'b1': jnp.zeros((L, 4 * D), dtype=jnp.float32), 'W2': jax.random.normal(ks[5], (L, 4 * D, D), dtype=jnp.float32) * (1.0 / np.sqrt(4 * D)), 'b2': jnp.zeros((L, D), dtype=jnp.float32), 'g1': jnp.ones((L, D), dtype=jnp.float32), 'beta1': jnp.zeros((L, D), dtype=jnp.float32), 'g2': jnp.ones((L, D), dtype=jnp.float32), 'beta2': jnp.zeros((L, D), dtype=jnp.float32)}
    _L0_gnn_all = _L0_gnn_setup()
    _L0_gnn_in = {k: v for k, v in _L0_gnn_all.items() if k in ('attn_w', 'attn_b', 'W1', 'b1', 'W2', 'b2', 'g1', 'beta1', 'g2', 'beta2')}
    del _L0_gnn_all
    return {'x': x, 'adj': adj, 'L0_gnn_attn_w': _L0_gnn_in['attn_w'], 'L0_gnn_attn_b': _L0_gnn_in['attn_b'], 'L0_gnn_W1': _L0_gnn_in['W1'], 'L0_gnn_b1': _L0_gnn_in['b1'], 'L0_gnn_W2': _L0_gnn_in['W2'], 'L0_gnn_b2': _L0_gnn_in['b2'], 'L0_gnn_g1': _L0_gnn_in['g1'], 'L0_gnn_beta1': _L0_gnn_in['beta1'], 'L0_gnn_g2': _L0_gnn_in['g2'], 'L0_gnn_beta2': _L0_gnn_in['beta2']}

def reference(x, adj, L0_gnn_attn_w, L0_gnn_attn_b, L0_gnn_W1, L0_gnn_b1, L0_gnn_W2, L0_gnn_b2, L0_gnn_g1, L0_gnn_beta1, L0_gnn_g2, L0_gnn_beta2):
    import jax
    import jax.numpy as jnp

    def _L0_gnn_ref(node_features, adjacency_matrix, attn_w, attn_b, W1, b1, W2, b2, g1, beta1, g2, beta2):
        import jax, jax.numpy as jnp
        import numpy as np
        L = 3
        D = 256
        B, N = (8, 512)
        EPS = 1e-05

        def layernorm(x, gamma, beta):
            mu = jnp.mean(x, axis=-1, keepdims=True)
            var = jnp.var(x, axis=-1, keepdims=True)
            return (x - mu) * jax.lax.rsqrt(var + EPS) * gamma + beta
        n = adjacency_matrix.shape[-1]
        mask = adjacency_matrix.astype(jnp.float32) + jnp.eye(n, dtype=jnp.float32) > 0
        x = node_features
        d = x.shape[-1]
        for l in range(attn_w.shape[0]):
            si = x @ attn_w[l, :d]
            sj = x @ attn_w[l, d:]
            scores = si[:, :, None] + sj[:, None, :] + attn_b[l]
            scores = jnp.where(scores >= 0, scores, 0.2 * scores)
            scores = jnp.where(mask, scores, -jnp.inf)
            attn = jax.nn.softmax(scores, axis=-1)
            agg = jnp.einsum('bij,bjd->bid', attn, x)
            h = layernorm(x + agg, g1[l], beta1[l])
            ff = jax.nn.gelu(h @ W1[l] + b1[l], approximate=False) @ W2[l] + b2[l]
            x = layernorm(h + ff, g2[l], beta2[l])
        return x
    h = jnp.maximum(_layernorm(x, axis=-1), 0.0)
    x = x + _L0_gnn_ref(h, adj, L0_gnn_attn_w, L0_gnn_attn_b, L0_gnn_W1, L0_gnn_b1, L0_gnn_W2, L0_gnn_b2, L0_gnn_g1, L0_gnn_beta1, L0_gnn_g2, L0_gnn_beta2)
    return x

_drawn_inputs = setup_inputs


def setup_inputs(seed=0):
    import zlib

    import numpy as np

    out = dict(_drawn_inputs(seed))
    spreads = {'L0_gnn_b1': (0.0, 0.1),
     'L0_gnn_b2': (0.0, 0.1),
     'L0_gnn_g1': (1.0, 0.2),
     'L0_gnn_beta1': (0.0, 0.1),
     'L0_gnn_g2': (1.0, 0.2),
     'L0_gnn_beta2': (0.0, 0.1)}
    factors = {'L0_gnn_attn_b': 192.224}
    for name, (base, spread) in spreads.items():
        noise = np.random.default_rng([zlib.crc32(name.encode()), seed]).standard_normal(out[name].shape)
        drawn = base * np.exp(spread * noise) if base else spread * noise
        out[name] = jnp.asarray(drawn.astype(out[name].dtype))
    for name, factor in factors.items():
        out[name] = (out[name] * factor).astype(out[name].dtype)
    return out
```

```python
import concourse.bass as bass
from concourse import mybir
from contextlib import ExitStack


def gnn_kernel(nc, x, adj, attn_w, attn_b, W1, b1, W2, b2, g1, beta1, g2, beta2, out):
    f32, f16, bf16 = mybir.dt.float32, mybir.dt.float16, mybir.dt.bfloat16
    i32, u8 = mybir.dt.int32, mybir.dt.uint8
    ALU, ACT, AX = mybir.AluOpType, mybir.ActivationFunctionType, mybir.AxisListType
    RMAX = bass.bass_isa.ReduceOp.max

    B, N, D = x.shape
    L, F = b1.shape
    P = 128
    NT, DT, FT = N // P, D // P, F // P
    NC, CT = 2, NT // 2
    CN = CT * P
    PAIRS = B // 2
    EPS, SLOPE = 1e-5, 0.2
    OUTSIDE = -3.0e38
    PSCALE = 128.0
    WN = DT * F

    x_v = x.rearrange("b (t p) d -> b p t d", p=P)
    out_v = out.rearrange("b (t p) d -> b p t d", p=P)
    adj_v = adj.rearrange("b (t p) n -> b t p n", p=P)
    W1_v = W1.rearrange("l (c p) f -> l p c f", p=P)
    W2_v = W2.rearrange("l (c p) d -> l p c d", p=P)
    halves_dram = nc.dram_tensor("weight_halves", [L, P, 4 * WN], f16, kind="Internal").ap()

    ctx = ExitStack()
    with ctx:
        def sb(name, shape, dt):
            return ctx.enter_context(nc.sbuf_tensor(name, shape, dt))

        def sem(name):
            return ctx.enter_context(nc.semaphore(name))

        X = [sb(f"X{s}", [P, NT, D], f32) for s in range(2)]
        XH = [sb(f"XH{s}", [P, NT, D + 1], f16) for s in range(2)]
        XL = [sb(f"XL{s}", [P, NT, D], f16) for s in range(2)]
        BIAS = [sb(f"BIAS{s}", [P, NT, N], bf16) for s in range(2)]
        MASK = [sb(f"MASK{s}", [P, NT, N], u8) for s in range(2)]
        PH = sb("PH", [P, NT, N], f16)
        PL = sb("PL", [P, NT, N], f16)
        HTH = sb("HTH", [P, DT, CN], f16)
        HTL = sb("HTL", [P, DT, CN], f16)
        GR = 4
        GH = sb("GH", [P, GR, CN], f16)
        GL = sb("GL", [P, GR, CN], f16)
        GF = sb("GF", [P, 2, CN], f32)
        WS = sb("WS", [P, 4, WN], f16)
        E = sb("E", [P, 4, N], f32)
        ADJ = sb("ADJ", [P, 2, N], i32)
        XO = sb("XO", [P, CT, D], f32)
        ROWS = sb("ROWS", [P, 7, L * D], f32)
        G1, BE1, G2, BE2, WI, WJ, B2 = range(7)
        B1 = sb("B1", [P, L * FT], f32)
        AB = sb("AB", [P, L], f32)
        AB2 = sb("AB2", [P, 1], f32)
        IDF = sb("IDF", [P, P], f32)
        IDB = sb("IDB", [P, P], bf16)
        KP = 3 * 2 * NT
        SEL = sb("SEL", [KP, 2 * NT, P], bf16)
        NHALF = sb("NHALF", [P, CT], f32)
        JUNKN = sb("JUNKN", [P, N], bf16)
        JUNK = JUNKN[:, 0:2 * D].bitcast(f32)
        DIAG = sb("DIAG", [P, P], f32)
        SI = [sb(f"SI{s}", [P, NT], f32) for s in range(2)]
        SJ = [sb(f"SJ{s}", [P, NT], f32) for s in range(2)]
        SJS = [sb(f"SJS{s}", [P, NT], f32) for s in range(2)]
        MX = sb("MX", [P, NT], f32)
        T1 = sb("T1", [P, NT], f32)
        T2 = sb("T2", [P, NT], f32)
        UV = sb("UV", [P, 2, NT], f32)
        REST = sb("REST", [P, 2, NT], f32)
        PARTW = sb("PARTW", [P, P], bf16)
        PARTS = PARTW[:, 0:KP].rearrange("p (a b c) -> p a b c", a=3, b=2)
        PT = sb("PT", [KP, P], bf16)
        RC = sb("RC", [P, 2], f32)
        BN = sb("BN", [P, NT, 6], f32)
        MV = sb("MV", [P, NT, 2], f32)
        MVB = sb("MVB", [P, NT, 2], f32)
        VE = sb("VE", [P, CT], f32)
        EPSC = sb("EPSC", [P, CT], f32)
        RS = sb("RS", [P, NT], f32)
        RSB = sb("RSB", [P, NT], f32)
        NMR = sb("NMR", [P, NT], f32)
        MAXES = sb("MAXES", [P, 7], f32)
        MAXED = sb("MAXED", [P, 7], f32)
        BOUND = sb("BOUND", [P, 5], f32)
        K = 10
        AW1, AW2, AH, AG, AXN, D1, D2, IAX, AB_, ABN = range(K)
        LC = sb("LC", [P, L * K], f32)
        VC = sb("VC", [P, K], f32)
        SC = sb("SC", [P, K], f32)
        SB1 = sb("SB1", [P, FT], f32)
        VW = sb("VW", [P, 2, D], f32)
        PB2 = sb("PB2", [P, D], f32)
        AX0 = sb("AX0", [P, 1], f32)
        INV = sb("INV", [P, 5], f32)
        R = ctx.enter_context(nc.psum_tensor("R", [P, 4 * 512], f32))
        FB = [ctx.enter_context(nc.psum_tensor(f"FB{i}", [P, 512], f32)) for i in range(2)]
        AC = [ctx.enter_context(nc.psum_tensor(f"AC{i}", [P, 512], f32)) for i in range(2)]
        RU, RV = R[:, 0:N], R[:, N:2 * N]
        RT = R[:, N:N + P // 2].bitcast(bf16)
        RM = [R[:, 512 * i:512 * i + 512].bitcast(bf16) for i in range(4)]

        const_in, const_ready = sem("const_in"), sem("const_ready")
        raw_in, maxes_ready, maxed, halves_ready, halves_out = (
            sem(n) for n in ("raw_in", "maxes_ready", "maxed", "halves_ready", "halves_out"))
        w1_in, w2_in = sem("w1_in"), sem("w2_in")
        x_in = [sem(f"x_in{s}") for s in range(2)]
        adj_in = [sem(f"adj_in{i}") for i in range(2)]
        adj_used, bias_ready, mask_turned, mask_ready = (
            sem(n) for n in ("adj_used", "bias_ready", "mask_turned", "mask_ready"))
        batch_var, batch_rstd, batch_norm = sem("batch_var"), sem("batch_rstd"), sem("batch_norm")
        xo_in, xo_sum, out_done = sem("xo_in"), sem("xo_sum"), sem("out_done")
        acc_full, acc_free = sem("acc_full"), sem("acc_free")
        f_full, f_free = sem("f_full"), sem("f_free")
        var_ready, rstd_ready = sem("var_ready"), sem("rstd_ready")
        h_ready, h_biased = sem("h_ready"), sem("h_biased")
        ht_hi, ht_lo = sem("ht_hi"), sem("ht_lo")
        g_hi, g_lo, ff2_done = sem("g_hi"), sem("g_lo"), sem("ff2_done")
        x_ready, x_hi, x_lo = sem("x_ready"), sem("x_hi"), sem("x_lo")
        parts_ready, parts_turned, turned_ready, rows_ready = (
            sem(n) for n in ("parts_ready", "parts_turned", "turned_ready", "rows_ready"))
        exps = sem("exps")
        p_f, p_hi, p_lo = sem("p_f"), sem("p_hi"), sem("p_lo")
        v_chain, a_chain, g_chain = sem("v_chain"), sem("a_chain"), sem("g_chain")

        ACC_N, FB_N = NT + 2 * NC, NC * (DT + FT)
        FULL_N = NT + NC
        FF_N = NC * FT

        def need(eng, s, v):
            if not (isinstance(v, int) and v <= 0):
                eng.wait_ge(s, v)

        def row(k, l):
            return ROWS[:, k, bass.ds(l * D, D)]

        def steps(eng, body):
            with eng.Fori(0, PAIRS) as p:
                with eng.Fori(0, L - 1) as l:
                    body(p, l, L * p + l, False)
                body(p, L - 1, L * p + (L - 1), True)

        block = ctx.enter_context(nc.Block())

        @block.sync
        def _(sp):
            for k, t in ((G1, g1), (BE1, beta1), (B2, b2), (G2, g2), (BE2, beta2)):
                sp.dma_start(ROWS[:, k, :], t.rearrange("l d -> (l d)").partition_broadcast(P)).then_inc(const_in, 16)
            for k, c in ((WI, 0), (WJ, D)):
                sp.dma_start(ROWS[:, k, :].rearrange("p (l d) -> p l d", l=L),
                             attn_w[:, c:c + D].partition_broadcast(P)).then_inc(const_in, 16)
            with nc.allow_non_contiguous_dma(reason="a few kilobytes of biases, once"):
                sp.dma_start(B1[:, :].rearrange("p (l f) -> p l f", l=L),
                             b1.rearrange("l (f p) -> p l f", p=P)).then_inc(const_in, 16)
            sp.dma_start(AB[:, :], attn_b.partition_broadcast(P)).then_inc(const_in, 16)

            def load_adj(v, b):
                for r in range(NT):
                    need(sp, adj_used, NT * v + r - 1)
                    sp.dma_start(ADJ[:, r % 2, :], adj_v[b, r]).then_inc(adj_in[r % 2], 16)

            for l in range(L):
                need(sp, halves_ready, l)
                sp.dma_start(E[:, 0:2, :], W1_v[l]).then_inc(raw_in, 16)
                sp.dma_start(E[:, 2:4, :].rearrange("p a (c d) -> p (a c) d", d=D), W2_v[l]).then_inc(raw_in, 16)
                if l == 0:
                    for s in range(2):
                        sp.dma_start(X[s][:, :, :], x_v[s]).then_inc(x_in[s], 16)
                if l >= 1:
                    sp.wait_ge(halves_ready, l)
                    sp.dma_start(halves_dram[l - 1], (PH if l % 2 else PL)[:, :, :]).then_inc(halves_out, 16)
            sp.wait_ge(halves_ready, L)
            sp.dma_start(halves_dram[L - 1], (PH if L % 2 else PL)[:, :, :]).then_inc(halves_out, 16)
            sp.wait_ge(halves_out, 16 * L)
            for s in range(2):
                load_adj(s, s)

            def body(p, l, it, last):
                need(sp, f_free, 2 * FB_N * it + 2)
                sp.dma_start(WS[:, 0:2, :], halves_dram[bass.ds(l, 1), :, 0:2 * WN]).then_inc(w1_in, 16)
                need(sp, ff2_done, 2 * FF_N * it + GR)
                sp.dma_start(WS[:, 2:4, :], halves_dram[bass.ds(l, 1), :, 2 * WN:4 * WN]).then_inc(w2_in, 16)
                if last:
                    nxt = (p + 1) % PAIRS
                    for s in range(2):
                        load_adj(2 * p + s + 2, bass.ds(2 * nxt + s, 1))
                        for c in range(NC):
                            ts = slice(CT * c, CT * c + CT)
                            done = 2 * (2 * p + s) + c
                            sp.dma_start(XO[:, :, :], x_v[bass.ds(2 * p + s, 1), :, ts, :]).then_inc(xo_in, 16)
                            sp.wait_ge(xo_sum, done + 1)
                            sp.dma_start(out_v[bass.ds(2 * p + s, 1), :, ts, :], XO[:, :, :]).then_inc(out_done, 16)
                            sp.wait_ge(out_done, 16 * done + 16)
                        sp.dma_start(X[s][:, :, :], x_v[bass.ds(2 * nxt + s, 1)]).then_inc(x_in[s], 16)

            steps(sp, body)

        @block.gpsimd
        def _(pool):
            n = [0]

            def link(ins):
                n[0] += 1
                ins.then_inc(g_chain, 1)
                pool.wait_ge(g_chain, n[0])

            link(pool.memset(IDF[:, :], 0.0))
            link(pool.memset(IDB[:, :], 0.0))
            link(pool.memset(SEL[:, :, :], 0.0))
            for t in (IDF, IDB):
                pool.affine_select(out=t[:, :], in_=t[:, :], compare_op=ALU.not_equal, fill=1.0,
                                   base=0, pattern=[[-1, P]], channel_multiplier=1).then_inc(const_ready, 1)
            for m in range(3):
                link(pool.affine_select(out=SEL[:, :, :], in_=SEL[:, :, :], compare_op=ALU.not_equal, fill=1.0,
                                        base=-2 * NT * m, pattern=[[-1, 2 * NT], [0, P]], channel_multiplier=1))
            for s in range(2):
                pool.memset(XH[s][:, :, D:D + 1], 1.0).then_inc(const_ready, 1)
            link(pool.memset(NHALF[:, :], -0.5))
            pool.memset(EPSC[:, :], EPS).then_inc(const_ready, 1)

            for l in range(L):
                pool.wait_ge(maxes_ready, l + 1)
                pool.partition_all_reduce(MAXED[:, :], MAXES[:, :], P, RMAX).then_inc(maxed, 1)

            def rstd(mv, rs, c, ready, n_ready, done):
                pool.wait_ge(ready, n_ready)
                link(pool.tensor_tensor(VE[:, :], mv[:, CT * c:CT * c + CT, 1], EPSC[:, :], ALU.add))
                pool.tensor_tensor(rs[:, CT * c:CT * c + CT], VE[:, :], NHALF[:, :], ALU.pow).then_inc(done, 1)
                pool.wait_ge(done, n_ready)

            def batch(v):
                for c in range(NC):
                    rstd(MVB, RSB, c, batch_var, NC * v + c + 1, batch_rstd)

            pool.wait_ge(const_ready, 5)
            pool.wait_ge(const_in, 16 * 9)
            for v in range(2):
                batch(v)

            def body(p, l, it, last):
                pool.sem_clear(g_chain)
                n[0] = 0
                link(pool.tensor_copy(PB2[:, :], row(B2, l)))
                for s in range(2):
                    U = 2 * it + s

                    def biased(c):
                        pool.wait_ge(f_full, FB_N * U + (DT + FT) * c + DT)
                        xs = X[s][:, CT * c:CT * c + CT, :]
                        pool.tensor_tensor(xs, xs, PB2[:, :].unsqueeze(1).to_broadcast([P, CT, D]),
                                           ALU.add).then_inc(h_biased, 1)

                    rstd(MV, RS, 0, var_ready, 4 * U + 1, rstd_ready)
                    rstd(MV, RS, 1, var_ready, 4 * U + 2, rstd_ready)
                    biased(0)
                    biased(1)
                    for c in range(NC):
                        rstd(MV, RS, c, var_ready, 4 * U + 3 + c, rstd_ready)
                        if last:
                            done = 2 * (2 * p + s) + c
                            pool.wait_ge(xo_in, 16 * done + 16)
                            pool.wait_ge(x_ready, 2 * U + c + 1)
                            pool.tensor_tensor(XO[:, :, :], XO[:, :, :], X[s][:, CT * c:CT * c + CT, :],
                                               ALU.add).then_inc(xo_sum, 1)
                    if last:
                        batch(2 * p + s + 2)

            steps(pool, body)

        @block.scalar
        def _(act):
            n = [0]

            def link(ins):
                n[0] += 1
                ins.then_inc(a_chain, 1)
                act.wait_ge(a_chain, n[0])

            def x_upper(s, c, ready, n_ready):
                act.wait_ge(ready, n_ready)
                ts = slice(CT * c, CT * c + CT)
                act.activation(XH[s][:, ts, 0:D], X[s][:, ts, :], ACT.Copy, scale=SC[:, AXN:AXN + 1]).then_inc(x_hi, 1)

            def batch_rows(s, v):
                for c in range(NC):
                    act.wait_ge(batch_norm, NC * v + c + 1)
                    for t in range(CT * c, CT * c + CT):
                        ins = act.activation(X[s][:, t, :], X[s][:, t, :], ACT.Relu,
                                             bias=NMR[:, t:t + 1], scale=RSB[:, t:t + 1])
                    link(ins)
                    ts = slice(CT * c, CT * c + CT)
                    act.activation(XH[s][:, ts, 0:D], X[s][:, ts, :], ACT.Copy, scale=AX0[:, :]).then_inc(x_hi, 1)

            def batch_mask(s, v):
                for j in range(NT):
                    act.wait_ge(mask_turned, NT * v + j + 1)
                    act.activation(MASK[s][:, j, :], RM[j % 4], ACT.Relu, bias=PCOL).then_inc(mask_ready, 1)

            PCOL = AB2[:, 0:1]

            def exp_tile(s, k, j):
                e = 2 * (j % 2)
                act.wait_ge(p_lo, NT * k + j + 1)
                act.activation(E[:, e, :], RU, ACT.Exp, bias=SJ[s][:, j:j + 1]).then_inc(exps, 1)
                act.activation(E[:, e + 1, :], RV, ACT.Exp, bias=SJS[s][:, j:j + 1]).then_inc(exps, 1)

            def p_upper(k, j):
                act.wait_ge(p_f, NT * k + j + 1)
                if j == 0:
                    need(act, acc_full, FULL_N * (k - 1) + NT)
                act.activation(PH[:, j, :], E[:, 2 * (j % 2), :], ACT.Copy).then_inc(p_hi, 1)

            def weights(s, k, js):
                if js[0] == 0:
                    act.wait_ge(rows_ready, 2 * k + 2)
                exp_tile(s, k, js[0])
                exp_tile(s, k, js[1])
                for j in js[2:]:
                    p_upper(k, j - 2)
                    exp_tile(s, k, j)
                p_upper(k, js[-2])
                p_upper(k, js[-1])

            act.wait_ge(const_in, 16 * 9)
            act.wait_ge(const_ready, 5)
            for v in range(2):
                batch_rows(v, v)
            for v in range(2):
                batch_mask(v, v)
            weights(0, 0, list(range(0, 4)))
            weights(0, 0, list(range(4, 8)))

            def body(p, l, it, last):
                act.sem_clear(a_chain)
                n[0] = 0
                act.wait_ge(x_hi, 4 * it + 4)
                act.activation(SB1[:, :], B1[:, bass.ds(l * FT, FT)], ACT.Copy)
                link(act.activation(SC[:, :], LC[:, bass.ds(l * K, K)], ACT.Copy))
                for s in range(2):
                    U = 2 * it + s

                    def ht_upper(c):
                        for d in range(DT):
                            act.wait_ge(f_full, FB_N * U + (DT + FT) * c + d + 1)
                            act.activation(HTH[:, d, :], FB[d % 2][:, :], ACT.Copy,
                                           scale=SC[:, AH:AH + 1]).then_inc(ht_hi, 1)

                    def gelu(c, f):
                        k = FT * c + f
                        act.wait_ge(f_full, FB_N * U + (DT + FT) * c + DT + f + 1)
                        act.wait_ge(g_lo, FF_N * U + k + 1)
                        ins = act.activation(GF[:, k % 2, :], FB[f % 2][:, :], ACT.Gelu,
                                             bias=SB1[:, f:f + 1], scale=SC[:, D1:D1 + 1])
                        ins.then_inc(f_free, 1)
                        act.wait_ge(f_free, FB_N * U + (DT + FT) * c + DT + f + 3)
                        act.wait_ge(ff2_done, FF_N * U + k + 1)
                        act.activation(GH[:, k % GR, :], GF[:, k % 2, :], ACT.Copy,
                                       scale=SC[:, AG:AG + 1]).then_inc(g_hi, 1)

                    ht_upper(0)
                    weights(1 - s, U + 1, list(range(0, 4)))
                    for f in range(FT):
                        gelu(0, f)
                    ht_upper(1)
                    weights(1 - s, U + 1, list(range(4, 8)))
                    for f in range(FT):
                        gelu(1, f)
                        if f == 2 and not last:
                            x_upper(s, 0, x_ready, 2 * U + 1)
                    if last:
                        batch_rows(s, 2 * p + s + 2)
                        batch_mask(s, 2 * p + s + 2)
                    else:
                        x_upper(s, 1, x_ready, 2 * U + 2)

            steps(act, body)

        @block.tensor
        def _(pe):
            def turn_parts(k, half, masks):
                pe.wait_ge(parts_ready, 2 * k + half + 1)
                if half == 0:
                    need(pe, exps, 2 * NT * k)
                    need(pe, mask_ready, masks)
                pe.transpose(RT, PARTW[:, :], IDB[:, :]).then_inc(parts_turned, 1)

            def spread(k, half):
                pe.wait_ge(turned_ready, 2 * k + half + 1)
                for q in range(2 * NT if half else NT):
                    ins = pe.matmul(R[:, q * P:(q + 1) * P], SEL[:, q, :], PT[:, :], start=True, stop=True)
                ins.then_inc(rows_ready, 1)

            def batch_mask(s, v, k):
                pe.wait_ge(bias_ready, NT * v + NT)
                for j in range(NT):
                    if j == 0:
                        need(pe, exps, 2 * NT * k)
                    need(pe, mask_ready, NT * v + j - 3)
                    for r in range(NT):
                        ins = pe.transpose(RM[j % 4][:, r * P:(r + 1) * P], BIAS[s][:, r, j * P:(j + 1) * P],
                                           IDB[:, :])
                    ins.then_inc(mask_turned, 1)

            pe.wait_ge(const_ready, 5)
            for v in range(2):
                batch_mask(v, v, 0)
            for half in range(2):
                turn_parts(0, half, NT * 2)
                spread(0, half)

            def body(p, l, it, last):
                for s in range(2):
                    U = 2 * it + s

                    def attend(t):
                        if t == 0:
                            pe.wait_ge(x_hi, 2 * U + 2)
                            pe.wait_ge(x_lo, 2 * U + 2)
                            pe.wait_ge(p_hi, NT * (U + 1))
                            pe.wait_ge(p_lo, NT * (U + 1) + 2)
                        pe.wait_ge(acc_free, ACC_N * U + t + 1)
                        ac = AC[t % 2]
                        for j in range(NT):
                            ph, pl = PH[:, j, t * P:(t + 1) * P], PL[:, j, t * P:(t + 1) * P]
                            pe.matmul(ac[:, 0:D + 1], ph, XH[s][:, j, :], start=(j == 0), stop=False)
                            pe.matmul(ac[:, 0:D], ph, XL[s][:, j, :], start=False, stop=False,
                                      skip_group_check=True)
                            ins = pe.matmul(ac[:, 0:D + 1], pl, XH[s][:, j, :], start=False, stop=(j == NT - 1),
                                            skip_group_check=(j < NT - 1))
                        ins.then_inc(acc_full, 1)

                    def turn_h(c):
                        pe.wait_ge(h_ready, 2 * U + c + 1)
                        for d in range(DT):
                            pe.wait_ge(f_free, FB_N * U + (DT + FT) * c + d + 1)
                            for t in range(CT):
                                ins = pe.transpose(FB[d % 2][:, t * P:(t + 1) * P],
                                                   X[s][:, CT * c + t, d * P:(d + 1) * P], IDF[:, :])
                            ins.then_inc(f_full, 1)

                    def first(c, f):
                        if f == 0:
                            pe.wait_ge(ht_hi, 4 * U + 2 * c + 2)
                            pe.wait_ge(ht_lo, 4 * U + 2 * c + 2)
                            if s == 0 and c == 0:
                                pe.wait_ge(w1_in, 16 * it + 16)
                        pe.wait_ge(f_free, FB_N * U + (DT + FT) * c + DT + f + 1)
                        for d in range(DT):
                            cols = slice(d * F + f * P, d * F + (f + 1) * P)
                            hh, hl = HTH[:, d, :], HTL[:, d, :]
                            pe.matmul(FB[f % 2][:, :], WS[:, 0, cols], hh, start=(d == 0), stop=False)
                            pe.matmul(FB[f % 2][:, :], WS[:, 0, cols], hl, start=False, stop=False)
                            ins = pe.matmul(FB[f % 2][:, :], WS[:, 1, cols], hh, start=False, stop=(d == DT - 1))
                        ins.then_inc(f_full, 1)

                    def second(c, f):
                        k = FT * c + f
                        if f == 0:
                            pe.wait_ge(acc_free, ACC_N * U + NT + 2 * c + 2)
                            if s == 0 and c == 0:
                                pe.wait_ge(w2_in, 16 * it + 16)
                        pe.wait_ge(g_hi, FF_N * U + k + 1)
                        pe.wait_ge(g_lo, FF_N * U + k + 3)
                        wh, wl = (WS[:, a, f * D:(f + 1) * D] for a in (2, 3))
                        for t in (range(CT) if f < FT - 1 else (1, 0, 3, 2)):
                            ac = AC[t // 2][:, (t % 2) * D:(t % 2 + 1) * D]
                            gh, gl = (g[:, k % GR, t * P:(t + 1) * P] for g in (GH, GL))
                            pe.matmul(ac, gh, wh, start=(f == 0 and t % 2 == 0), stop=False,
                                      skip_group_check=not (f == 0 and t % 2 == 0))
                            pe.matmul(ac, gh, wl, start=False, stop=False, skip_group_check=True)
                            end = f == FT - 1 and t % 2 == 0
                            ins = pe.matmul(ac, gl, wh, start=False, stop=end, skip_group_check=not end)
                            if f == FT - 1 and t == 0:
                                ins.then_inc(acc_full, 1)
                        ins.then_inc(ff2_done, 1)

                    masks = NT * (2 * p + 2) + (NT if last and s else 0)
                    attend(0)
                    turn_parts(U + 1, 0, masks)
                    attend(1)
                    spread(U + 1, 0)
                    for t in range(2, 6):
                        attend(t)
                    turn_h(0)
                    attend(6)
                    turn_parts(U + 1, 1, masks)
                    attend(7)
                    spread(U + 1, 1)
                    for c in range(NC):
                        first(c, 0)
                        for f in range(1, FT):
                            first(c, f)
                            second(c, f - 1)
                        if c == 0:
                            turn_h(1)
                        second(c, FT - 1)
                    if last:
                        batch_mask(s, 2 * p + s + 2, U + 2)

            steps(pe, body)

        @block.vector
        def _(dve):
            n = [0]

            def link(ins):
                n[0] += 1
                ins.then_inc(v_chain, 1)
                dve.wait_ge(v_chain, n[0])

            def split_parts():
                link(dve.tensor_copy(PARTS[:, 0], UV[:, :, :]))
                link(dve.tensor_tensor(REST[:, :, :], UV[:, :, :], PARTS[:, 0], ALU.subtract))
                link(dve.tensor_copy(PARTS[:, 1], REST[:, :, :]))
                link(dve.tensor_tensor(REST[:, :, :], REST[:, :, :], PARTS[:, 1], ALU.subtract))
                dve.tensor_copy(PARTS[:, 2], REST[:, :, :]).then_inc(parts_ready, 1)

            def node_parts(s, k):
                need(dve, parts_turned, 2 * k)
                link(dve.tensor_copy(UV[:, 0, :], SJ[s][:, :]))
                split_parts()

            def turned(k, half):
                dve.wait_ge(parts_turned, 2 * k + half + 1)
                dve.tensor_copy(PT[:, :], RT[0:KP, :]).then_inc(turned_ready, 1)

            def row_max(s, k, t):
                if t == 0:
                    dve.wait_ge(rows_ready, 2 * k + 1)
                link(dve.tensor_tensor_reduce(JUNKN[:, :], RU, BIAS[s][:, t, :], 1.0, OUTSIDE, ALU.add, ALU.max,
                                              MX[:, t:t + 1]))

            def row_parts(s, k, ab):
                link(dve.tensor_scalar(T1[:, :], SI[s][:, :], ab, None, ALU.add))
                link(dve.tensor_tensor(T2[:, :], T1[:, :], MX[:, :], ALU.add))
                link(dve.scalar_tensor_tensor(T2[:, :], T2[:, :], SLOPE, T2[:, :], ALU.mult, ALU.max))
                dve.tensor_tensor(UV[:, 0, :], T1[:, :], T2[:, :], ALU.subtract)
                link(dve.scalar_tensor_tensor(UV[:, 1, :], T1[:, :], SLOPE, T2[:, :], ALU.mult, ALU.subtract))
                split_parts()

            def weight(s, k, j):
                e = 2 * (j % 2)
                dve.wait_ge(exps, 2 * NT * k + 2 * j + 2)
                link(dve.tensor_tensor(E[:, e, :], E[:, e, :], E[:, e + 1, :], ALU.max))
                if j == 0:
                    pass
                dve.scalar_tensor_tensor(E[:, e, :], E[:, e, :], 1.0, MASK[s][:, j, :], ALU.min,
                                         ALU.mult).then_inc(p_f, 1)

            def p_lower(k, j):
                dve.wait_ge(p_hi, NT * k + j + 1)
                dve.tensor_tensor(PL[:, j, :], E[:, 2 * (j % 2), :], PH[:, j, :], ALU.subtract).then_inc(p_lo, 1)

            def node_scores(s, c):
                for t in range(CT * c, CT * c + CT):
                    for k, to in ((0, SI), (1, SJ)):
                        link(dve.tensor_tensor_reduce(JUNK, X[s][:, t, :], VW[:, k, :], 1.0, 0.0, ALU.mult,
                                                      ALU.add, to[s][:, t:t + 1]))
                cs = slice(CT * c, CT * c + CT)
                link(dve.tensor_scalar(SJS[s][:, cs], SJ[s][:, cs], SLOPE, None, ALU.mult))

            def x_lower(s, c, ax, count):
                dve.wait_ge(x_hi, count)
                ts = slice(CT * c, CT * c + CT)
                dve.scalar_tensor_tensor(XL[s][:, ts, :], X[s][:, ts, :], ax, XH[s][:, ts, 0:D],
                                         ALU.mult, ALU.subtract).then_inc(x_lo, 1)

            def stats(s, t, mv, done=None):
                link(dve.bn_stats(BN[:, t, :], X[s][:, t, :]))
                link(dve.bn_aggr(mv[:, t, :], BN[:, t, :]))
                if done is not None:
                    dve.sem_inc(done, 1)

            def batch_bias(s, v, r):
                dve.wait_ge(adj_in[r % 2], 16 * (NT // 2) * v + 16 * (r // 2 + 1))
                link(dve.tensor_scalar(BIAS[s][:, r, :], ADJ[:, r % 2, :], 0.0, OUTSIDE, ALU.is_le, ALU.mult))
                blk = slice(r * P, (r + 1) * P)
                link(dve.tensor_tensor(DIAG[:, :], ADJ[:, r % 2, blk], IDF[:, :], ALU.add))
                dve.sem_inc(adj_used, 1)
                dve.tensor_scalar(BIAS[s][:, r, blk], DIAG[:, :], 0.0, OUTSIDE, ALU.is_le,
                                  ALU.mult).then_inc(bias_ready, 1)

            def batch_rows(s, v, loads, tail):
                dve.wait_ge(x_in[s], loads)
                for c in range(NC):
                    for t in range(CT * c, CT * c + CT):
                        stats(s, t, MVB, batch_var if t % CT == CT - 1 else None)
                for c in range(NC):
                    cs = slice(CT * c, CT * c + CT)
                    dve.wait_ge(batch_rstd, NC * v + c + 1)
                    dve.scalar_tensor_tensor(NMR[:, cs], MVB[:, cs, 0], -1.0, RSB[:, cs], ALU.mult,
                                             ALU.mult).then_inc(batch_norm, 1)
                for c in range(NC):
                    x_lower(s, c, AX0[:, :], NC * tail + c + 1)
                    node_scores(s, c)

            dve.memset(AB2[:, :], PSCALE).then_inc(v_chain, 1)
            n[0] += 1
            dve.sem_inc(acc_free, 2)
            dve.sem_inc(f_free, 2)
            dve.sem_inc(g_lo, 2)
            dve.sem_inc(ff2_done, GR)
            dve.sem_inc(p_lo, 2)
            link(dve.memset(UV[:, :, :], 0.0))
            link(dve.memset(PARTW[:, :], 0.0))
            link(dve.memset(AX0[:, :], 2.0 ** 9))
            link(dve.memset(LC[:, IAX:IAX + 1], 2.0 ** -9))
            dve.wait_ge(const_in, 16 * 9)
            dve.wait_ge(const_ready, 5)

            for l in range(L):
                dve.wait_ge(raw_in, 32 * (l + 1))
                if l:
                    dve.wait_ge(maxed, l)
                w1, w2 = (E[:, 2 * a:2 * a + 2, :].rearrange("p a n -> p (a n)") for a in range(2))

                def biggest(k, src):
                    return dve.tensor_reduce(MAXES[:, k:k + 1], src, AX.X, ALU.max, apply_absolute_value=True)

                biggest(0, w1)
                biggest(1, w2)
                biggest(2, row(G1, l))
                biggest(3, row(BE1, l))
                biggest(4, B1[:, FT * l:FT * l + FT])
                biggest(5, row(G2, l))
                biggest(6, row(BE2, l)).then_inc(maxes_ready, 1)
                dve.wait_ge(maxed, l + 1)

                def at(k, l=l):
                    return LC[:, K * l + k:K * l + k + 1]

                root = float(D) ** 0.5
                link(dve.tensor_copy(BOUND[:, 0:2], MAXED[:, 0:2]))
                link(dve.scalar_tensor_tensor(BOUND[:, AH:AH + 1], MAXED[:, 2:3], root, MAXED[:, 3:4],
                                              ALU.mult, ALU.add))
                link(dve.scalar_tensor_tensor(BOUND[:, AXN:AXN + 1], MAXED[:, 5:6], root, MAXED[:, 6:7],
                                              ALU.mult, ALU.add))
                link(dve.scalar_tensor_tensor(BOUND[:, AG:AG + 1], BOUND[:, AH:AH + 1], float(D), MAXED[:, 0:1],
                                              ALU.mult, ALU.mult))
                link(dve.tensor_tensor(BOUND[:, AG:AG + 1], BOUND[:, AG:AG + 1], MAXED[:, 4:5], ALU.add))
                link(dve.tensor_scalar(BOUND[:, :], BOUND[:, :], 1e-12, None, ALU.max))
                link(dve.tensor_scalar(BOUND[:, :].bitcast(i32), BOUND[:, :].bitcast(i32), 0x7F800000, None,
                                       ALU.bitwise_and))
                link(dve.reciprocal(INV[:, :], BOUND[:, :]))
                sc = LC[:, K * l:K * l + 5]
                link(dve.tensor_scalar(sc, INV[:, :], 2.0 ** 13, None, ALU.mult))
                link(dve.tensor_tensor(at(D1), at(AW1), at(AH), ALU.mult))
                link(dve.tensor_tensor(at(D2), at(AW2), at(AG), ALU.mult))
                link(dve.reciprocal(at(D1), at(D1)))
                link(dve.reciprocal(at(D2), at(D2)))
                if l < L - 1:
                    link(dve.reciprocal(at(IAX, l + 1), at(AXN)))
                link(dve.tensor_copy(at(AB_), AB[:, l:l + 1]))
                link(dve.tensor_copy(at(ABN), AB[:, (l + 1) % L:(l + 1) % L + 1]))
                ST = PL if l % 2 else PH
                if l >= 2:
                    dve.wait_ge(halves_out, 16 * (l - 1))
                for a, w in enumerate((w1, w2)):
                    hi, lo = (ST[:, 4 * a + 2 * h:4 * a + 2 * h + 2, :].rearrange("p a n -> p (a n)")
                              for h in range(2))
                    link(dve.tensor_scalar(hi, w, sc[:, a:a + 1], None, ALU.mult))
                    link(dve.scalar_tensor_tensor(lo, w, sc[:, a:a + 1], hi, ALU.mult, ALU.subtract))
                dve.sem_inc(halves_ready, 1)

            link(dve.tensor_copy(VW[:, :, :], ROWS[:, WI:WJ + 1, 0:D]))
            for v in range(2):
                batch_rows(v, v, 16, v)
            for v in range(2):
                for r in range(NT):
                    batch_bias(v, v, r)

            node_parts(0, 0)
            turned(0, 0)
            for t in range(NT):
                row_max(0, 0, t)
            row_parts(0, 0, AB[:, 0:1])
            turned(0, 1)
            dve.wait_ge(mask_ready, NT * 2)
            dve.wait_ge(halves_out, 16 * L)
            for j in range(NT):
                weight(0, 0, j)
                p_lower(0, j)

            def body(p, l, it, last):
                dve.sem_clear(v_chain)
                n[0] = 0
                dve.wait_ge(x_lo, 4 * it + 4)
                dve.tensor_copy(VC[:, :], LC[:, bass.ds(l * K, K)])
                link(dve.tensor_copy(VW[:, :, :], ROWS[:, WI:WJ + 1, bass.ds(0 if last else (l + 1) * D, D)]))
                for s in range(2):
                    U, o = 2 * it + s, 1 - s
                    ab = VC[:, AB_:AB_ + 1] if s == 0 else VC[:, ABN:ABN + 1]

                    def attended(t):
                        dve.wait_ge(acc_full, FULL_N * U + t + 1)
                        ac = AC[t % 2]
                        link(dve.reciprocal(RC[:, 0:1], ac[:, D:D + 1]))
                        link(dve.tensor_scalar(RC[:, 1:2], RC[:, 0:1], VC[:, IAX:IAX + 1], None, ALU.mult))
                        link(dve.scalar_tensor_tensor(X[s][:, t, :], ac[:, 0:D], RC[:, 1:2], X[s][:, t, :],
                                                      ALU.mult, ALU.add))
                        dve.sem_inc(acc_free, 1)
                        stats(s, t, MV, var_ready if t % CT == CT - 1 else None)

                    def normed(c, g, b, count, done):
                        dve.wait_ge(rstd_ready, count)
                        for t in range(CT * c, CT * c + CT):
                            ins = dve.scalar_tensor_tensor(X[s][:, t, :], X[s][:, t, :], MV[:, t, 0:1], row(g, l),
                                                           ALU.subtract, ALU.mult)
                        link(ins)
                        for t in range(CT * c, CT * c + CT):
                            ins = dve.scalar_tensor_tensor(X[s][:, t, :], X[s][:, t, :], RS[:, t:t + 1], row(b, l),
                                                           ALU.mult, ALU.add)
                        ins.then_inc(done, 1)
                        dve.wait_ge(done, 2 * U + c + 1)

                    def ht_lower(c):
                        for d in range(DT):
                            dve.wait_ge(ht_hi, 4 * U + 2 * c + d + 1)
                            link(dve.scalar_tensor_tensor(HTL[:, d, :], FB[d % 2][:, :], VC[:, AH:AH + 1],
                                                          HTH[:, d, :], ALU.mult, ALU.subtract))
                            dve.sem_inc(ht_lo, 1)
                            dve.sem_inc(f_free, 1)

                    def gelu_lower(c, f):
                        k = FT * c + f
                        dve.wait_ge(g_hi, FF_N * U + k + 1)
                        dve.scalar_tensor_tensor(GL[:, k % GR, :], GF[:, k % 2, :], VC[:, AG:AG + 1],
                                                 GH[:, k % GR, :], ALU.mult, ALU.subtract).then_inc(g_lo, 1)

                    def fed(c):
                        dve.wait_ge(h_biased, 2 * U + c + 1)
                        for q in range(CT):
                            t = CT * c + q
                            if q < 2:
                                dve.wait_ge(acc_full, FULL_N * U + NT + c + 1)
                            else:
                                dve.wait_ge(ff2_done, FF_N * U + FT * (c + 1) + GR)
                            link(dve.scalar_tensor_tensor(X[s][:, t, :], AC[q // 2][:, (q % 2) * D:(q % 2 + 1) * D],
                                                          VC[:, D2:D2 + 1], X[s][:, t, :], ALU.mult, ALU.add))
                            if q % 2:
                                dve.sem_inc(acc_free, 1)
                        for q in range(CT):
                            stats(s, CT * c + q, MV, var_ready if q == CT - 1 else None)

                    def tail(c):
                        normed(c, G2, BE2, 4 * U + 3 + c, x_ready)
                        if not last:
                            node_scores(s, c)

                    def lower(c):
                        if not last:
                            x_lower(s, c, VC[:, AXN:AXN + 1], 2 * (U + 2) + c + 1)

                    node_parts(o, U + 1)
                    attended(0)
                    turned(U + 1, 0)
                    attended(1)
                    row_max(o, U + 1, 0)
                    row_max(o, U + 1, 1)
                    attended(2)
                    row_max(o, U + 1, 2)
                    row_max(o, U + 1, 3)
                    attended(3)
                    normed(0, G1, BE1, 4 * U + 1, h_ready)
                    attended(4)
                    row_max(o, U + 1, 4)
                    row_max(o, U + 1, 5)
                    attended(5)
                    row_max(o, U + 1, 6)
                    row_max(o, U + 1, 7)
                    row_parts(o, U + 1, ab)
                    ht_lower(0)
                    attended(6)
                    turned(U + 1, 1)
                    attended(7)
                    normed(1, G1, BE1, 4 * U + 2, h_ready)
                    dve.wait_ge(mask_ready, NT * (2 * p + 2) + (NT if last and s else 0))
                    for j in range(4):
                        weight(o, U + 1, j)
                        if j:
                            p_lower(U + 1, j - 1)
                    p_lower(U + 1, 3)
                    for f in range(FT):
                        gelu_lower(0, f)
                    ht_lower(1)
                    fed(0)
                    for j in range(4, 8):
                        weight(o, U + 1, j)
                        if j > 4:
                            p_lower(U + 1, j - 1)
                    p_lower(U + 1, 7)
                    tail(0)
                    for f in range(FT):
                        gelu_lower(1, f)
                        if last:
                            batch_bias(s, 2 * p + s + 2, f)
                        if f == 3:
                            lower(0)
                    fed(1)
                    tail(1)
                    lower(1)
                    if last:
                        batch_rows(s, 2 * p + s + 2, 16 * (p + 2), U + 2)

            steps(dve, body)


_INS = ['x', 'adj', 'L0_gnn_attn_w', 'L0_gnn_attn_b', 'L0_gnn_W1', 'L0_gnn_b1', 'L0_gnn_W2', 'L0_gnn_b2',
        'L0_gnn_g1', 'L0_gnn_beta1', 'L0_gnn_g2', 'L0_gnn_beta2']
_OUTS = [((8, 1024, 256), 'float32')]


def kernel(**inputs):
    import numpy as _np
    import concourse.bacc as _bacc
    from concourse import mybir as _mybir
    from concourse.bass_utils import run_bass_kernel_spmd as _run

    nc = _bacc.Bacc("TRN2", target_bir_lowering=False, num_devices=1)
    arrays, args = {}, []
    for name in _INS:
        a = _np.ascontiguousarray(inputs[name])
        arrays[f"in_{name}_dram"] = a
        args.append(nc.dram_tensor(f"in_{name}_dram", a.shape, _mybir.dt.from_np(a.dtype), kind="ExternalInput").ap())
    for i, (shape, dtype) in enumerate(_OUTS):
        dt = _mybir.dt.from_np(_np.dtype(dtype))
        args.append(nc.dram_tensor(f"out_{i}_dram", shape, dt, kind="ExternalOutput").ap())
    gnn_kernel(nc, *args)
    r = _run(nc, [arrays], core_ids=[0])
    got = tuple(r.results[0][f"out_{i}_dram"] for i in range(len(_OUTS)))
    return got[0]
```

```python
import concourse.bass as bass
from concourse import mybir
from contextlib import ExitStack


def gnn_kernel(nc, x, adj, attn_w, attn_b, W1, b1, W2, b2, g1, beta1, g2, beta2, out):
    f32, f16, bf16 = mybir.dt.float32, mybir.dt.float16, mybir.dt.bfloat16
    i32, u8 = mybir.dt.int32, mybir.dt.uint8
    ALU, ACT, AX = mybir.AluOpType, mybir.ActivationFunctionType, mybir.AxisListType
    RMAX = bass.bass_isa.ReduceOp.max

    B, N, D = x.shape
    L, F = b1.shape
    P = 128
    NT, DT, FT = N // P, D // P, F // P
    NC, CT = 2, NT // 2
    CN = CT * P
    PAIRS = B // 2
    EPS, SLOPE = 1e-5, 0.2
    OUTSIDE = -3.0e38
    PSCALE = 128.0
    WN = DT * F

    x_v = x.rearrange("b (t p) d -> b p t d", p=P)
    out_v = out.rearrange("b (t p) d -> b p t d", p=P)
    adj_v = adj.rearrange("b (t p) n -> b t p n", p=P)
    W1_v = W1.rearrange("l (c p) f -> l p c f", p=P)
    W2_v = W2.rearrange("l (c p) d -> l p c d", p=P)
    halves_dram = nc.dram_tensor("weight_halves", [L, P, 4 * WN], f16, kind="Internal").ap()

    ctx = ExitStack()
    with ctx:
        def sb(name, shape, dt):
            return ctx.enter_context(nc.sbuf_tensor(name, shape, dt))

        def sem(name):
            return ctx.enter_context(nc.semaphore(name))

        X = [sb(f"X{s}", [P, NT, D], f32) for s in range(2)]
        XH = [sb(f"XH{s}", [P, NT, D + 1], f16) for s in range(2)]
        XL = [sb(f"XL{s}", [P, NT, D], f16) for s in range(2)]
        BIAS = [sb(f"BIAS{s}", [P, NT, N], bf16) for s in range(2)]
        MASK = [sb(f"MASK{s}", [P, NT, N], u8) for s in range(2)]
        PH = sb("PH", [P, NT, N], f16)
        PL = sb("PL", [P, NT, N], f16)
        HTH = sb("HTH", [P, DT, CN], f16)
        HTL = sb("HTL", [P, DT, CN], f16)
        GR = 4
        GH = sb("GH", [P, GR, CN], f16)
        GL = sb("GL", [P, GR, CN], f16)
        WS = sb("WS", [P, 4, WN], f16)
        ER = 5
        E = sb("E", [P, ER, N], f32)
        US = sb("US", [P, N], f32)
        ADJ = sb("ADJ", [P, 2, N], i32)
        XO = sb("XO", [P, CT, D], f32)
        ROWS = sb("ROWS", [P, 6, L * D], f32)
        G1, BB, G2, BE2, WI, WJ = range(6)
        B1 = sb("B1", [P, L * FT], f32)
        GB1 = sb("GB1", [P, 2, L * DT], f32)
        AB = sb("AB", [P, L], f32)
        AB2 = sb("AB2", [P, 1], f32)
        RAW = [E[:, 0:4, :].rearrange("p a n -> p (a n)"),
               BIAS[0][:, :, :].rearrange("p a n -> p (a n)").bitcast(f32)]
        XN = ADJ[:, :, :].bitcast(f32).rearrange("p a n -> p (a n)").rearrange("p (t d) -> p t d", d=D)
        IDF = sb("IDF", [P, P], f32)
        IDB = sb("IDB", [P, P], bf16)
        KP = 3 * 2 * NT
        SEL = sb("SEL", [KP, 2 * NT, P], bf16)
        NHALF = sb("NHALF", [P, CT], f32)
        JUNKN = sb("JUNKN", [P, N], bf16)
        JUNK = [JUNKN[:, 2 * D * i:2 * D * (i + 1)].bitcast(f32) for i in range(2)]
        DIAG = sb("DIAG", [P, P], f32)
        SI = [sb(f"SI{s}", [P, NT], f32) for s in range(2)]
        SJ = [sb(f"SJ{s}", [P, NT], f32) for s in range(2)]
        SJS = [sb(f"SJS{s}", [P, NT], f32) for s in range(2)]
        MX = sb("MX", [P, NT], f32)
        T1 = sb("T1", [P, NT], f32)
        T2 = sb("T2", [P, NT], f32)
        UV = sb("UV", [P, 2, NT], f32)
        REST = sb("REST", [P, 2, NT], f32)
        PARTW = sb("PARTW", [P, P], bf16)
        PARTS = PARTW[:, 0:KP].rearrange("p (a b c) -> p a b c", a=3, b=2)
        PT = sb("PT", [KP, P], bf16)
        RC = sb("RC", [P, NT], f32)
        BN = sb("BN", [P, NT, 6], f32)
        MV = sb("MV", [P, NT, 2], f32)
        MVB = sb("MVB", [P, NT, 2], f32)
        VE = sb("VE", [P, CT], f32)
        EPSC = sb("EPSC", [P, CT], f32)
        RS = sb("RS", [P, NT], f32)
        RSB = sb("RSB", [P, NT], f32)
        NMR = sb("NMR", [P, NT], f32)
        NMB = sb("NMB", [P, NT], f32)
        MAXES = sb("MAXES", [P, 7], f32)
        MAXED = sb("MAXED", [P, 7], f32)
        BOUND = sb("BOUND", [P, 5], f32)
        K = 10 + DT
        AW1, AW2, AH, AG, AXN, AXE, D1, D2, AB_, ABN, GS = range(11)
        LC = sb("LC", [P, L * K], f32)
        VC = sb("VC", [P, K], f32)
        SC = sb("SC", [P, K], f32)
        SB1 = sb("SB1", [P, FT], f32)
        VW = sb("VW", [P, 2, D], f32)
        AX0 = sb("AX0", [P, 1], f32)
        INV = sb("INV", [P, 5], f32)
        R = ctx.enter_context(nc.psum_tensor("R", [P, 4 * 512], f32))
        FB = [ctx.enter_context(nc.psum_tensor(f"FB{i}", [P, 512], f32)) for i in range(2)]
        AC = [ctx.enter_context(nc.psum_tensor(f"AC{i}", [P, 512], f32)) for i in range(2)]
        RU, RV = R[:, 0:N], R[:, N:2 * N]
        RT = R[:, N:N + P // 2].bitcast(bf16)
        RM = [R[:, N + 512 * i:N + 512 * i + 512].bitcast(bf16) for i in range(2)]

        const_in, const_ready = sem("const_in"), sem("const_ready")
        raw_in = [sem(f"raw_in{i}") for i in range(2)]
        maxes_ready, maxed, halves_ready = (
            sem(n) for n in ("maxes_ready", "maxed", "halves_ready"))
        halves_out = [sem(f"halves_out{i}") for i in range(2)]
        w1_in, w2_in = sem("w1_in"), sem("w2_in")
        x_in = [sem(f"x_in{s}") for s in range(2)]
        adj_in = [sem(f"adj_in{i}") for i in range(2)]
        adj_used, bias_ready, mask_turned, mask_ready = (
            sem(n) for n in ("adj_used", "bias_ready", "mask_turned", "mask_ready"))
        batch_var, batch_rstd, batch_norm = sem("batch_var"), sem("batch_rstd"), sem("batch_norm")
        batch_relu, xn_in, beta_done = sem("batch_relu"), sem("xn_in"), sem("beta_done")
        scales_ready, w_hi = sem("scales_ready"), sem("w_hi")
        batch_scored, sp_steps = sem("batch_scored"), sem("sp_steps")
        xo_in, xo_sum, out_done = sem("xo_in"), sem("xo_sum"), sem("out_done")
        acc_full, acc_free = sem("acc_full"), sem("acc_free")
        f_full, f_free = sem("f_full"), sem("f_free")
        var_ready, rstd_ready = sem("var_ready"), sem("rstd_ready")
        nmr_ready, n_ready, r_ready, scored = (
            sem(k) for k in ("nmr_ready", "n_ready", "r_ready", "scored"))
        ht_hi = sem("ht_hi")
        g_hi, ff2_done = sem("g_hi"), sem("ff2_done")
        x_final, x_hi, x_lo = sem("x_final"), sem("x_hi"), sem("x_lo")
        parts_ready, parts_turned, turned_ready, rows_ready = (
            sem(n) for n in ("parts_ready", "parts_turned", "turned_ready", "rows_ready"))
        exps, e_max, u_copied = sem("exps"), sem("e_max"), sem("u_copied")
        p_f, p_hi, p_lo = sem("p_f"), sem("p_hi"), sem("p_lo")
        v_chain, a_chain, g_chain = sem("v_chain"), sem("a_chain"), sem("g_chain")

        ACC_N, FB_N = NT - 2 + 2 * NC, 2 + NC * (DT + FT)
        FULL_N, FF1_N = NT + NC, NC * (DT + FT)
        CONSTS = 11

        def h_use(c, d):
            return 2 + (DT + FT) * c + d

        def f_use(c, f):
            return 2 + (DT + FT) * c + DT + f

        WIDE = f_use(0, 4)

        def f_bank(i):
            return FB[i % 2] if i < WIDE or i % 4 < 2 else R[:, 512 * (i % 2):512 * (i % 2) + 512]

        def f_before(i):
            return (i - 2 if i < WIDE + 2 else i - 4) + 1 + 2
        VWB = E[:, 4, 0:L * D]
        FF_N = NC * FT

        def half_place(l, a, h):
            return (PL if l % 2 else PH)[:, 4 * a + 2 * h:4 * a + 2 * h + 2, :].rearrange("p a n -> p (a n)")

        def need(eng, s, v):
            if not (isinstance(v, int) and v <= 0):
                eng.wait_ge(s, v)

        def row(k, l):
            return ROWS[:, k, bass.ds(l * D, D)]

        def steps(eng, body):
            with eng.Fori(0, PAIRS) as p:
                with eng.Fori(0, L - 1) as l:
                    body(p, l, L * p + l, False)
                body(p, L - 1, L * p + (L - 1), True)

        block = ctx.enter_context(nc.Block())

        @block.sync
        def _(sp):
            for k, t in ((G1, g1), (BB, beta1), (G2, g2), (BE2, beta2)):
                sp.dma_start(ROWS[:, k, :], t.rearrange("l d -> (l d)").partition_broadcast(P)).then_inc(const_in, 16)
            sp.dma_start(VWB[:, :], b2.rearrange("l d -> (l d)").partition_broadcast(P)).then_inc(const_in, 16)
            for k, c in ((WI, 0), (WJ, D)):
                sp.dma_start(ROWS[:, k, :].rearrange("p (l d) -> p l d", l=L),
                             attn_w[:, c:c + D].partition_broadcast(P)).then_inc(const_in, 16)
            with nc.allow_non_contiguous_dma(reason="a few kilobytes of biases, once"):
                sp.dma_start(B1[:, :].rearrange("p (l f) -> p l f", l=L),
                             b1.rearrange("l (f p) -> p l f", p=P)).then_inc(const_in, 16)
                for k, t in ((0, g1), (1, beta1)):
                    sp.dma_start(GB1[:, k, :].rearrange("p (l c) -> p l c", l=L),
                                 t.rearrange("l (c p) -> p l c", p=P)).then_inc(const_in, 16)
            sp.dma_start(AB[:, :], attn_b.partition_broadcast(P)).then_inc(const_in, 16)

            def load_adj(v, b, free=0, tiles=range(NT)):
                for r in tiles:
                    if r >= free:
                        need(sp, adj_used, NT * v + r - 1)
                    sp.dma_start(ADJ[:, r % 2, :], adj_v[b, r]).then_inc(adj_in[r % 2], 16)

            def store_halves(l):
                sp.wait_ge(halves_ready, l + 1)
                sp.dma_start(halves_dram[l], (PL if l % 2 else PH)[:, :, :]).then_inc(halves_out[l % 2], 16)

            for l in range(L):
                need(sp, halves_ready, l - 1)
                for a, (w, k) in enumerate(((W1_v, DT), (W2_v, FT))):
                    sp.dma_start(RAW[l % 2][:, a * WN:(a + 1) * WN].rearrange("p (c f) -> p c f", c=k),
                                 w[l]).then_inc(raw_in[l % 2], 16)
                if l == 1:
                    for s in range(2):
                        sp.dma_start(X[s][:, :, :], x_v[s]).then_inc(x_in[s], 16)
                    load_adj(0, 0, tiles=range(0, 2))
                if l >= 2:
                    store_halves(l - 2)
            for l in range(max(L - 2, 0), L):
                store_halves(l)
            load_adj(0, 0, tiles=range(2, NT))
            load_adj(1, 1)
            for i in range(2):
                sp.wait_ge(halves_out[i], 16 * ((L - i + 1) // 2))

            def body(p, l, it, last):
                need(sp, f_free, 2 * FB_N * it + 2)
                sp.dma_start(WS[:, 0:2, :], halves_dram[bass.ds(l, 1), :, 0:2 * WN]).then_inc(w1_in, 16)
                need(sp, ff2_done, 2 * FF_N * it + GR)
                sp.dma_start(WS[:, 2:4, :], halves_dram[bass.ds(l, 1), :, 2 * WN:4 * WN]).then_inc(w2_in, 16)
                if last:
                    nxt = (p + 1) % PAIRS
                    for s in range(2):
                        def load_xo(c):
                            sp.wait_ge(out_done, 16 * (2 * (2 * p + s) + c) + 16)
                            sp.dma_start(XO[:, :, :], x_v[bass.ds(2 * p + s, 1), :,
                                                          CT * c:CT * c + CT, :]).then_inc(xo_in, 16)

                        def store_xo(c):
                            sp.wait_ge(xo_sum, 2 * (2 * p + s) + c + 1)
                            sp.dma_start(out_v[bass.ds(2 * p + s, 1), :, CT * c:CT * c + CT, :],
                                         XO[:, :, :]).then_inc(out_done, 16)

                        load_xo(0)
                        sp.wait_ge(batch_scored, 2 * p + s + 2)
                        sp.sem_inc(sp_steps, 1)
                        sp.wait_ge(x_final, 2 * it + 1 + 2 * s)
                        load_adj(2 * p + s + 2, bass.ds(2 * nxt + s, 1), free=2)
                        sp.wait_ge(adj_used, NT * (2 * p + s + 3))
                        sp.dma_start(XN, x_v[bass.ds(2 * nxt + s, 1)]).then_inc(xn_in, 16)
                        store_xo(0)
                        load_xo(1)
                        store_xo(1)

            sp.sem_inc(out_done, 16)
            steps(sp, body)
            sp.wait_ge(out_done, 16 * (B * NC + 1))

        @block.gpsimd
        def _(pool):
            n = [0]

            def link(ins):
                n[0] += 1
                ins.then_inc(g_chain, 1)
                pool.wait_ge(g_chain, n[0])

            link(pool.memset(IDF[:, :], 0.0))
            link(pool.memset(IDB[:, :], 0.0))
            link(pool.memset(SEL[:, :, :], 0.0))
            for t in (IDF, IDB):
                pool.affine_select(out=t[:, :], in_=t[:, :], compare_op=ALU.not_equal, fill=1.0,
                                   base=0, pattern=[[-1, P]], channel_multiplier=1).then_inc(const_ready, 1)
            for m in range(3):
                link(pool.affine_select(out=SEL[:, :, :], in_=SEL[:, :, :], compare_op=ALU.not_equal, fill=1.0,
                                        base=-2 * NT * m, pattern=[[-1, 2 * NT], [0, P]], channel_multiplier=1))
            for s in range(2):
                pool.memset(XH[s][:, :, D:D + 1], 1.0).then_inc(const_ready, 1)
            link(pool.memset(NHALF[:, :], -0.5))
            pool.memset(EPSC[:, :], EPS).then_inc(const_ready, 1)

            for l in range(L):
                pool.wait_ge(maxes_ready, l + 1)
                pool.partition_all_reduce(MAXED[:, :], MAXES[:, :], P, RMAX).then_inc(maxed, 1)

            def rstd(mv, rs, c, ready, n_ready, done):
                pool.wait_ge(ready, n_ready)
                link(pool.tensor_tensor(VE[:, :], mv[:, CT * c:CT * c + CT, 1], EPSC[:, :], ALU.add))
                pool.tensor_tensor(rs[:, CT * c:CT * c + CT], VE[:, :], NHALF[:, :], ALU.pow).then_inc(done, 1)
                pool.wait_ge(done, n_ready)

            def spread_row(k, l):
                return row(k, l).unsqueeze(1).to_broadcast([P, CT, D])

            def batch(v):
                need(pool, batch_relu, NC * v)
                for c in range(NC):
                    rstd(MVB, RSB, c, batch_var, NC * v + c + 1, batch_rstd)

            pool.wait_ge(const_ready, 5)
            for v in range(2):
                batch(v)

            def p_lower(k, j):
                pool.wait_ge(p_hi, NT * k + j + 1)
                pool.tensor_tensor(PL[:, j, :], E[:, j % ER, :], PH[:, j, :], ALU.subtract).then_inc(p_lo, 1)

            for j in range(NT):
                p_lower(0, j)

            def body(p, l, it, last):
                pool.sem_clear(g_chain)
                n[0] = 0
                for s in range(2):
                    U = 2 * it + s

                    def affine(c, ready, n_ready, g, b, done):
                        xs = X[s][:, CT * c:CT * c + CT, :]
                        pool.wait_ge(ready, n_ready)
                        pool.sem_inc(g_chain, 1)
                        n[0] += 1
                        link(pool.tensor_tensor(xs, xs, spread_row(g, l), ALU.mult))
                        ins = pool.tensor_tensor(xs, xs, spread_row(b, l), ALU.add)
                        if done is None:
                            link(ins)
                        else:
                            ins.then_inc(done, 1)

                    def finished(c):
                        affine(c, scored, 2 * U + c + 1, G2, BE2, x_final if c == NC - 1 and not last else None)
                        if last:
                            done = 2 * (2 * p + s) + c
                            pool.wait_ge(xo_in, 16 * done + 16)
                            pool.tensor_tensor(XO[:, :, :], XO[:, :, :], X[s][:, CT * c:CT * c + CT, :],
                                               ALU.add).then_inc(xo_sum, 1)

                    rstd(MV, RS, 0, var_ready, 4 * U + 1, rstd_ready)
                    rstd(MV, RS, 1, var_ready, 4 * U + 2, rstd_ready)
                    affine(0, f_full, FF1_N * U + DT, G1, BB, r_ready)
                    for j in range(0, 4):
                        p_lower(U + 1, j)
                    rstd(MV, RS, 0, var_ready, 4 * U + 3, rstd_ready)
                    affine(1, f_full, FF1_N * U + (DT + FT) + DT, G1, BB, r_ready)
                    if last:
                        finished(0)
                    for j in range(4, 8):
                        p_lower(U + 1, j)
                    rstd(MV, RS, 1, var_ready, 4 * U + 4, rstd_ready)
                    if last:
                        batch(2 * p + s + 2)
                    else:
                        finished(0)
                        finished(1)

            steps(pool, body)

        @block.scalar
        def _(act):
            n = [0]

            def link(ins):
                n[0] += 1
                ins.then_inc(a_chain, 1)
                act.wait_ge(a_chain, n[0])

            PCOL = AB2[:, 0:1]

            def x_upper(s, k, ax):
                act.wait_ge(x_final, k + 1)
                act.activation(XH[s][:, :, D:D + 1], ax.unsqueeze(1).to_broadcast([P, NT, 1]), ACT.Copy)
                act.activation(XH[s][:, :, 0:D], X[s][:, :, :], ACT.Copy, scale=ax).then_inc(x_hi, 1)

            def batch_rows(v, rows):
                for c in range(NC):
                    act.wait_ge(batch_norm, NC * v + c + 1)
                    for t in range(CT * c, CT * c + CT):
                        ins = act.activation(rows[:, t, :], rows[:, t, :], ACT.Relu,
                                             bias=NMB[:, t:t + 1], scale=RSB[:, t:t + 1])
                    ins.then_inc(batch_relu, 1)

            def batch_mask(s, v, js):
                for j in js:
                    act.wait_ge(mask_turned, NT * v + j + 1)
                    act.activation(MASK[s][:, j, :], RM[j % 2], ACT.Relu, bias=PCOL).then_inc(mask_ready, 1)

            def copy_u(k):
                act.wait_ge(rows_ready, 2 * k + 2)
                need(act, e_max, NT * k)
                act.activation(US[:, :], RU, ACT.Copy).then_inc(u_copied, 1)

            def exp_tile(s, k, j):
                act.wait_ge(e_max, NT * k + j + 1)
                act.activation(E[:, j % ER, :], E[:, j % ER, :], ACT.Exp, bias=SJ[s][:, j:j + 1]).then_inc(exps, 1)

            def p_upper(k, j):
                act.wait_ge(p_f, NT * k + j + 1)
                act.activation(PH[:, j, :], E[:, j % ER, :], ACT.Copy).then_inc(p_hi, 1)

            act.wait_ge(const_in, 16 * CONSTS)
            act.wait_ge(const_ready, 5)
            for l in range(L):
                act.wait_ge(scales_ready, l + 1)
                if l >= 2:
                    act.wait_ge(halves_out[l % 2], 16 * (l // 2))
                for a in range(2):
                    act.activation(half_place(l, a, 0), RAW[l % 2][:, a * WN:(a + 1) * WN], ACT.Copy,
                                   scale=LC[:, K * l + a:K * l + a + 1]).then_inc(w_hi, 1)
            for v in range(2):
                batch_rows(v, X[v])
                act.wait_ge(batch_relu, NC * v + NC)
                act.sem_inc(x_final, 1)
            act.wait_ge(batch_relu, NC * 2)
            x_upper(0, 0, AX0[:, :])
            for v in range(2):
                batch_mask(v, v, range(NT))
            copy_u(0)
            for js in (range(0, 4), range(4, 8)):
                for j in js:
                    exp_tile(0, 0, j)
                for j in js:
                    p_upper(0, j)

            def body(p, l, it, last):
                act.sem_clear(a_chain)
                n[0] = 0
                act.wait_ge(ff2_done, 2 * FF_N * it + GR)
                act.activation(SB1[:, :], B1[:, bass.ds(l * FT, FT)], ACT.Copy)
                link(act.activation(SC[:, :], LC[:, bass.ds(l * K, K)], ACT.Copy))
                for s in range(2):
                    U, o = 2 * it + s, 1 - s

                    def normed(c):
                        act.wait_ge(nmr_ready, 2 * U + c + 1)
                        for t in range(CT * c, CT * c + CT):
                            ins = act.activation(X[s][:, t, :], X[s][:, t, :], ACT.Identity,
                                                 bias=NMR[:, t:t + 1], scale=RS[:, t:t + 1])
                        ins.then_inc(n_ready, 1)

                    def ht_upper(c, d):
                        act.wait_ge(f_full, FF1_N * U + (DT + FT) * c + d + 1)
                        act.activation(HTH[:, d, :], f_bank(h_use(c, d))[:, :], ACT.Copy,
                                       scale=SC[:, GS + d:GS + d + 1]).then_inc(ht_hi, 1)

                    def gelu(c, f):
                        k = FT * c + f
                        act.wait_ge(f_full, FF1_N * U + (DT + FT) * c + DT + f + 1)
                        fb = f_bank(f_use(c, f))
                        link(act.activation(fb[:, :], fb[:, :], ACT.Gelu,
                                            bias=SB1[:, f:f + 1], scale=SC[:, D1:D1 + 1]))
                        act.wait_ge(ff2_done, FF_N * U + k + 1)
                        act.activation(GH[:, k % GR, :], fb[:, :], ACT.Copy,
                                       scale=SC[:, AG:AG + 1]).then_inc(g_hi, 1)

                    normed(0)
                    ht_upper(0, 0)
                    ht_upper(0, 1)
                    x_upper(o, U + 1, SC[:, AXN:AXN + 1] if s else SC[:, AXE:AXE + 1])
                    gelu(0, 0)
                    gelu(0, 1)
                    gelu(0, 2)
                    gelu(0, 3)
                    copy_u(U + 1)
                    gelu(0, 4)
                    for j in range(0, 4):
                        exp_tile(o, U + 1, j)
                    gelu(0, 5)
                    gelu(0, 6)
                    normed(1)
                    p_upper(U + 1, 0)
                    gelu(0, 7)
                    ht_upper(1, 0)
                    p_upper(U + 1, 1)
                    ht_upper(1, 1)
                    p_upper(U + 1, 2)
                    gelu(1, 0)
                    p_upper(U + 1, 3)
                    gelu(1, 1)
                    gelu(1, 2)
                    for j in range(4, 8):
                        exp_tile(o, U + 1, j)
                    gelu(1, 3)
                    for j in range(4, 8):
                        p_upper(U + 1, j)
                        gelu(1, j)
                        if last and j >= 6:
                            batch_mask(s, 2 * p + s + 2, range(0, 2) if j == 6 else range(2, 8))
                    if last:
                        batch_rows(2 * p + s + 2, XN)
                        act.wait_ge(xo_sum, 2 * (2 * p + s) + 2)
                        act.wait_ge(batch_relu, NC * (2 * p + s + 3))
                        act.activation(X[s][:, :, :], XN, ACT.Copy).then_inc(x_final, 1)

            steps(act, body)

        @block.tensor
        def _(pe):
            def turn_parts(k, half, masks):
                pe.wait_ge(parts_ready, 2 * k + half + 1)
                if half == 0:
                    need(pe, e_max, NT * k)
                    if not (isinstance(k, int) and k == 0):
                        pe.wait_ge(f_free, FB_N * (k - 1) + 2)
                    need(pe, mask_ready, masks)
                pe.transpose(RT, PARTW[:, :], IDB[:, :]).then_inc(parts_turned, 1)

            def spread(k, half):
                pe.wait_ge(turned_ready, 2 * k + half + 1)
                for q in range(2 * NT if half else NT):
                    ins = pe.matmul(R[:, q * P:(q + 1) * P], SEL[:, q, :], PT[:, :], start=True, stop=True)
                ins.then_inc(rows_ready, 1)

            def batch_mask(s, v, k, j):
                if j == 0:
                    pe.wait_ge(bias_ready, NT * v + NT)
                    need(pe, e_max, NT * k)
                need(pe, mask_ready, NT * v + j - 1)
                for r in range(NT):
                    ins = pe.transpose(RM[j % 2][:, r * P:(r + 1) * P], BIAS[s][:, r, j * P:(j + 1) * P], IDB[:, :])
                ins.then_inc(mask_turned, 1)

            pe.wait_ge(const_ready, 5)
            pe.wait_ge(const_in, 16 * CONSTS)
            for l in range(L):
                pe.wait_ge(raw_in[l % 2], 32 * (l // 2 + 1))
                for f in range(FT):
                    for d in range(DT):
                        ins = pe.matmul(FB[l % 2][:, f:f + 1], RAW[l % 2][:, d * F + f * P:d * F + (f + 1) * P],
                                        GB1[:, 1, DT * l + d:DT * l + d + 1], start=(d == 0), stop=(d == DT - 1))
                ins.then_inc(beta_done, 1)
            for v in range(2):
                for j in range(NT):
                    batch_mask(v, v, 0, j)
            for half in range(2):
                turn_parts(0, half, NT * 2)
                spread(0, half)

            def body(p, l, it, last):
                for s in range(2):
                    U = 2 * it + s

                    def attend(t):
                        if t == 0:
                            pe.wait_ge(x_hi, U + 1)
                            pe.wait_ge(x_lo, U + 1)
                            pe.wait_ge(p_hi, NT * (U + 1))
                            pe.wait_ge(p_lo, NT * (U + 1) + ER)
                        if t < 2:
                            pe.wait_ge(f_free, FB_N * U + t + 1)
                        else:
                            pe.wait_ge(acc_free, ACC_N * U + t - 1)
                        ac = (FB if t < 2 else AC)[t % 2]
                        for j in range(NT):
                            ph, pl = PH[:, j, t * P:(t + 1) * P], PL[:, j, t * P:(t + 1) * P]
                            pe.matmul(ac[:, 0:D + 1], ph, XH[s][:, j, :], start=(j == 0), stop=False)
                            pe.matmul(ac[:, 0:D], ph, XL[s][:, j, :], start=False, stop=False,
                                      skip_group_check=True)
                            ins = pe.matmul(ac[:, 0:D + 1], pl, XH[s][:, j, :], start=False, stop=(j == NT - 1),
                                            skip_group_check=(j < NT - 1))
                        ins.then_inc(acc_full, 1)

                    def turn_h(c, d):
                        if d == 0:
                            pe.wait_ge(n_ready, 2 * U + c + 1)
                        i = h_use(c, d)
                        pe.wait_ge(f_free, FB_N * U + f_before(i))
                        for t in range(CT):
                            ins = pe.transpose(f_bank(i)[:, t * P:(t + 1) * P],
                                               X[s][:, CT * c + t, d * P:(d + 1) * P], IDF[:, :])
                        ins.then_inc(f_full, 1)

                    def first(c, f):
                        if f == 0:
                            pe.wait_ge(ht_hi, 4 * U + 2 * c + 2)
                            if s == 0 and c == 0:
                                pe.wait_ge(w1_in, 16 * it + 16)
                        i = f_use(c, f)
                        if WIDE + 2 <= i < WIDE + 4:
                            pe.wait_ge(u_copied, U + 2)
                        else:
                            pe.wait_ge(f_free, FB_N * U + max(f_before(i), f_use(c, 0) + 2))
                        for d in range(DT):
                            cols = slice(d * F + f * P, d * F + (f + 1) * P)
                            hh, hl = HTH[:, d, :], HTL[:, d, :]
                            pe.matmul(f_bank(i)[:, :], WS[:, 0, cols], hh, start=(d == 0), stop=False)
                            pe.matmul(f_bank(i)[:, :], WS[:, 0, cols], hl, start=False, stop=False)
                            ins = pe.matmul(f_bank(i)[:, :], WS[:, 1, cols], hh, start=False, stop=(d == DT - 1))
                        ins.then_inc(f_full, 1)

                    def second(c, f):
                        k = FT * c + f
                        if f == 0:
                            pe.wait_ge(acc_free, ACC_N * U + NT + 2 * c)
                            if s == 0 and c == 0:
                                pe.wait_ge(w2_in, 16 * it + 16)
                        pe.wait_ge(g_hi, FF_N * U + k + 1)
                        pe.wait_ge(f_free, FB_N * U + f_use(c, f) + 3)
                        wh, wl = (WS[:, a, f * D:(f + 1) * D] for a in (2, 3))
                        for t in (range(CT) if f < FT - 1 else (1, 0, 3, 2)):
                            ac = AC[t // 2][:, (t % 2) * D:(t % 2 + 1) * D]
                            gh, gl = (g[:, k % GR, t * P:(t + 1) * P] for g in (GH, GL))
                            pe.matmul(ac, gh, wh, start=(f == 0 and t % 2 == 0), stop=False,
                                      skip_group_check=not (f == 0 and t % 2 == 0))
                            pe.matmul(ac, gh, wl, start=False, stop=False, skip_group_check=True)
                            end = f == FT - 1 and t % 2 == 0
                            ins = pe.matmul(ac, gl, wh, start=False, stop=end, skip_group_check=not end)
                            if f == FT - 1 and t == 0:
                                ins.then_inc(acc_full, 1)
                        ins.then_inc(ff2_done, 1)

                    masks = NT * (2 * p + 2) + (NT if last and s else 0)
                    for t in range(4):
                        attend(t)
                    turn_parts(U + 1, 0, masks)
                    spread(U + 1, 0)
                    attend(4)
                    attend(5)
                    turn_h(0, 0)
                    turn_h(0, 1)
                    attend(6)
                    first(0, 0)
                    first(0, 1)
                    attend(7)
                    first(0, 2)
                    second(0, 0)
                    second(0, 1)
                    first(0, 3)
                    turn_parts(U + 1, 1, masks)
                    spread(U + 1, 1)
                    for f in range(4, FT):
                        first(0, f)
                        second(0, f - 2)
                    turn_h(1, 0)
                    second(0, FT - 2)
                    turn_h(1, 1)
                    second(0, FT - 1)
                    for f in range(FT):
                        first(1, f)
                        if f >= 2 and f != 5:
                            second(1, f - 2 if f < 5 else f - 3)
                    for f in range(FT - 3, FT):
                        second(1, f)
                        if last and f < FT - 1:
                            for j in range(2 * (f - FT + 3), 2 * (f - FT + 3) + 2):
                                batch_mask(s, 2 * p + s + 2, U + 2, j)
                    if last:
                        for j in range(4, NT):
                            batch_mask(s, 2 * p + s + 2, U + 2, j)

            steps(pe, body)

        @block.vector
        def _(dve):
            n = [0]

            def mark(ins):
                n[0] += 1
                ins.then_inc(v_chain, 1)
                return n[0]

            def after(m):
                dve.wait_ge(v_chain, m)

            def link(ins):
                after(mark(ins))

            def split_parts():
                link(dve.tensor_copy(PARTS[:, 0], UV[:, :, :]))
                link(dve.tensor_tensor(REST[:, :, :], UV[:, :, :], PARTS[:, 0], ALU.subtract))
                link(dve.tensor_copy(PARTS[:, 1], REST[:, :, :]))
                link(dve.tensor_tensor(REST[:, :, :], REST[:, :, :], PARTS[:, 1], ALU.subtract))
                dve.tensor_copy(PARTS[:, 2], REST[:, :, :]).then_inc(parts_ready, 1)

            def node_parts(s, k):
                need(dve, parts_turned, 2 * k)
                link(dve.tensor_copy(UV[:, 0, :], SJ[s][:, :]))
                split_parts()

            def turned(k, half):
                dve.wait_ge(parts_turned, 2 * k + half + 1)
                dve.tensor_copy(PT[:, :], RT[0:KP, :]).then_inc(turned_ready, 1)

            def row_max(s, k, t):
                link(dve.tensor_tensor_reduce(JUNKN[:, :], RU, BIAS[s][:, t, :], 1.0, OUTSIDE, ALU.add, ALU.max,
                                              MX[:, t:t + 1]))

            def row_parts(s, k, ab):
                link(dve.tensor_scalar(T1[:, :], SI[s][:, :], ab, None, ALU.add))
                link(dve.tensor_tensor(T2[:, :], T1[:, :], MX[:, :], ALU.add))
                link(dve.scalar_tensor_tensor(T2[:, :], T2[:, :], SLOPE, T2[:, :], ALU.mult, ALU.max))
                dve.tensor_tensor(UV[:, 0, :], T1[:, :], T2[:, :], ALU.subtract)
                link(dve.scalar_tensor_tensor(UV[:, 1, :], T1[:, :], SLOPE, T2[:, :], ALU.mult, ALU.subtract))
                split_parts()

            def larger(s, k, j):
                if j == 0:
                    dve.wait_ge(u_copied, k + 1)
                if j == 0 or j >= ER:
                    dve.wait_ge(p_lo, NT * k + ER + max(j - ER + 1, 0))
                dve.scalar_tensor_tensor(E[:, j % ER, :], RV, SJS[s][:, j:j + 1], US[:, :], ALU.add,
                                         ALU.max).then_inc(e_max, 1)

            def masked(s, k, j):
                dve.wait_ge(exps, NT * k + j + 1)
                dve.scalar_tensor_tensor(E[:, j % ER, :], E[:, j % ER, :], 1.0, MASK[s][:, j, :], ALU.min,
                                         ALU.mult).then_inc(p_f, 1)

            def scores(s, t, rows, used):
                for k, to in ((0, SI), (1, SJ)):
                    if used[k]:
                        after(used[k])
                    used[k] = mark(dve.tensor_tensor_reduce(JUNK[k], rows[:, t, :], VW[:, k, :], 1.0, 0.0, ALU.mult,
                                                            ALU.add, to[s][:, t:t + 1]))

            def scores_end(s, c, done=None):
                after(n[0])
                cs = slice(CT * c, CT * c + CT)
                ins = dve.tensor_scalar(SJS[s][:, cs], SJ[s][:, cs], SLOPE - 1.0, None, ALU.mult)
                if done is None:
                    link(ins)
                else:
                    ins.then_inc(done, 1)

            def node_scores(s, c, rows, done=None):
                used = [n[0], n[0]]
                for t in range(CT * c, CT * c + CT):
                    scores(s, t, rows, used)
                scores_end(s, c, done)

            def x_lower(s, k, ax):
                dve.wait_ge(x_hi, k + 1)
                dve.scalar_tensor_tensor(XL[s][:, :, :], X[s][:, :, :], ax, XH[s][:, :, 0:D],
                                         ALU.mult, ALU.subtract).then_inc(x_lo, 1)

            def batch_bias(s, v, r):
                dve.wait_ge(adj_in[r % 2], 16 * (NT // 2) * v + 16 * (r // 2 + 1))
                link(dve.tensor_scalar(BIAS[s][:, r, :], ADJ[:, r % 2, :], 0.0, OUTSIDE, ALU.is_le, ALU.mult))
                blk = slice(r * P, (r + 1) * P)
                dve.tensor_tensor(DIAG[:, :], ADJ[:, r % 2, blk], IDF[:, :], ALU.add).then_inc(adj_used, 1)
                dve.wait_ge(adj_used, NT * v + r + 1)
                dve.tensor_scalar(BIAS[s][:, r, blk], DIAG[:, :], 0.0, OUTSIDE, ALU.is_le,
                                  ALU.mult).then_inc(bias_ready, 1)

            def batch_stats(v, rows):
                for c in range(NC):
                    ts = range(CT * c, CT * c + CT)
                    for t in ts:
                        m = mark(dve.bn_stats(BN[:, t, :], rows[:, t, :]))
                    after(m)
                    for t in ts:
                        ins = dve.bn_aggr(MVB[:, t, :], BN[:, t, :])
                    ins.then_inc(batch_var, 1)

            def batch_shift(v):
                need(dve, batch_relu, NC * v)
                for c in range(NC):
                    cs = slice(CT * c, CT * c + CT)
                    dve.wait_ge(batch_rstd, NC * v + c + 1)
                    dve.scalar_tensor_tensor(NMB[:, cs], MVB[:, cs, 0], -1.0, RSB[:, cs], ALU.mult,
                                             ALU.mult).then_inc(batch_norm, 1)

            def batch_scores(s, v, rows):
                for c in range(NC):
                    dve.wait_ge(batch_relu, NC * v + c + 1)
                    node_scores(s, c, rows, batch_scored if c == NC - 1 else None)

            dve.memset(AB2[:, :], PSCALE).then_inc(v_chain, 1)
            n[0] += 1
            dve.sem_inc(acc_free, 2)
            dve.sem_inc(f_free, 2)
            dve.sem_inc(ff2_done, GR)
            dve.sem_inc(p_lo, ER)
            link(dve.memset(UV[:, :, :], 0.0))
            link(dve.memset(PARTW[:, :], 0.0))
            link(dve.memset(AX0[:, :], 2.0 ** 9))
            dve.wait_ge(const_in, 16 * CONSTS)
            dve.wait_ge(const_ready, 5)

            for l in range(L):
                dve.wait_ge(raw_in[l % 2], 32 * (l // 2 + 1))
                if l:
                    dve.wait_ge(maxed, l)
                w1, w2 = (RAW[l % 2][:, a * WN:(a + 1) * WN] for a in range(2))

                def at(k, l=l):
                    return LC[:, K * l + k:K * l + k + 1]

                def biggest(k, src):
                    return dve.tensor_reduce(MAXES[:, k:k + 1], src, AX.X, ALU.max, apply_absolute_value=True)

                biggest(0, w1)
                biggest(1, w2)
                biggest(2, row(G1, l))
                biggest(3, row(BB, l))
                biggest(4, B1[:, FT * l:FT * l + FT])
                biggest(5, row(G2, l))
                biggest(6, row(BE2, l)).then_inc(maxes_ready, 1)
                dve.wait_ge(maxed, l + 1)
                root = float(D) ** 0.5
                link(dve.tensor_copy(BOUND[:, 0:2], MAXED[:, 0:2]))
                link(dve.scalar_tensor_tensor(BOUND[:, AH:AH + 1], MAXED[:, 2:3], root, MAXED[:, 3:4],
                                              ALU.mult, ALU.add))
                link(dve.scalar_tensor_tensor(BOUND[:, AXN:AXN + 1], MAXED[:, 5:6], root, MAXED[:, 6:7],
                                              ALU.mult, ALU.add))
                link(dve.scalar_tensor_tensor(BOUND[:, AG:AG + 1], BOUND[:, AH:AH + 1], float(D), MAXED[:, 0:1],
                                              ALU.mult, ALU.mult))
                link(dve.tensor_tensor(BOUND[:, AG:AG + 1], BOUND[:, AG:AG + 1], MAXED[:, 4:5], ALU.add))
                link(dve.tensor_scalar(BOUND[:, :], BOUND[:, :], 1e-12, None, ALU.max))
                link(dve.tensor_scalar(BOUND[:, AXN:AXN + 1], BOUND[:, AXN:AXN + 1], 0.25, None, ALU.max))
                link(dve.tensor_scalar(BOUND[:, :].bitcast(i32), BOUND[:, :].bitcast(i32), 0x7F800000, None,
                                       ALU.bitwise_and))
                link(dve.reciprocal(INV[:, :], BOUND[:, :]))
                sc = LC[:, K * l:K * l + 5]
                link(dve.tensor_scalar(sc, INV[:, :], 2.0 ** 13, None, ALU.mult))
                if l == L - 1:
                    link(dve.tensor_copy(at(AXN), AX0[:, :]))
                link(dve.tensor_copy(at(AXE), at(AXN, l - 1) if l else AX0[:, :]))
                link(dve.tensor_tensor(at(D1), at(AW1), at(AH), ALU.mult))
                link(dve.tensor_tensor(at(D2), at(AW2), at(AG), ALU.mult))
                link(dve.reciprocal(at(D1), at(D1)))
                link(dve.reciprocal(at(D2), at(D2)))
                link(dve.tensor_scalar(LC[:, K * l + GS:K * l + GS + DT], GB1[:, 0, DT * l:DT * l + DT], at(AH),
                                       None, ALU.mult))
                dve.wait_ge(beta_done, l + 1)
                b1l = B1[:, FT * l:FT * l + FT]
                link(dve.tensor_tensor(b1l, b1l, FB[l % 2][:, 0:FT], ALU.add))
                dve.sem_inc(scales_ready, 1)
                for a, w in enumerate((w1, w2)):
                    dve.wait_ge(w_hi, 2 * l + a + 1)
                    link(dve.scalar_tensor_tensor(half_place(l, a, 1), w, sc[:, a:a + 1], half_place(l, a, 0),
                                                  ALU.mult, ALU.subtract))
                dve.sem_inc(halves_ready, 1)

            link(dve.tensor_tensor(ROWS[:, BB, :], ROWS[:, BB, :], VWB, ALU.add))
            for l in range(1, L):
                for k in (WI, WJ):
                    link(dve.tensor_tensor_reduce(JUNK[0], row(k, l), row(BE2, l - 1), 1.0, 0.0, ALU.mult, ALU.add,
                                                  RC[:, 0:1]))
                    link(dve.tensor_tensor(AB[:, l:l + 1], AB[:, l:l + 1], RC[:, 0:1], ALU.add))
                    link(dve.tensor_tensor(row(k, l), row(k, l), row(G2, l - 1), ALU.mult))
            for l in range(L):
                link(dve.tensor_copy(LC[:, K * l + AB_:K * l + AB_ + 1], AB[:, l:l + 1]))
                link(dve.tensor_copy(LC[:, K * l + ABN:K * l + ABN + 1], AB[:, (l + 1) % L:(l + 1) % L + 1]))

            link(dve.tensor_copy(VW[:, :, :], ROWS[:, WI:WJ + 1, 0:D]))
            for v in range(2):
                dve.wait_ge(x_in[v], 16)
                batch_stats(v, X[v])
                batch_shift(v)
            for v in range(2):
                batch_scores(v, v, X[v])
            for v in range(2):
                for r in range(NT):
                    batch_bias(v, v, r)
            x_lower(0, 0, AX0[:, :])

            node_parts(0, 0)
            turned(0, 0)
            dve.wait_ge(rows_ready, 1)
            for t in range(NT):
                row_max(0, 0, t)
            row_parts(0, 0, AB[:, 0:1])
            turned(0, 1)
            dve.wait_ge(mask_ready, NT * 2)
            for i in range(2):
                dve.wait_ge(halves_out[i], 16 * ((L - i + 1) // 2))
            for js in (range(0, 4), range(4, 8)):
                for j in js:
                    larger(0, 0, j)
                for j in js:
                    masked(0, 0, j)

            def body(p, l, it, last):
                dve.sem_clear(v_chain)
                n[0] = 0
                dve.wait_ge(f_free, 2 * FB_N * it + 2)
                dve.tensor_copy(VC[:, :], LC[:, bass.ds(l * K, K)])
                link(dve.tensor_copy(VW[:, :, :], ROWS[:, WI:WJ + 1, bass.ds(0 if last else (l + 1) * D, D)]))
                for s in range(2):
                    U, o = 2 * it + s, 1 - s
                    k = U + 1
                    ab = VC[:, AB_:AB_ + 1] if s == 0 else VC[:, ABN:ABN + 1]

                    def stats(t, attend=False):
                        if attend:
                            if t < 2:
                                dve.wait_ge(f_free, FB_N * U + t + 3)
                            else:
                                dve.wait_ge(acc_free, ACC_N * U + t + 1)
                        return mark(dve.bn_stats(BN[:, t, :], X[s][:, t, :]))

                    def aggregate(t, m):
                        after(m)
                        ins = dve.bn_aggr(MV[:, t, :], BN[:, t, :])
                        if t % CT == CT - 1:
                            ins.then_inc(var_ready, 1)

                    def attended(t):
                        ac = (FB if t < 2 else AC)[t % 2]
                        dve.wait_ge(acc_full, FULL_N * U + t + 1)
                        m = mark(dve.reciprocal(RC[:, t:t + 1], ac[:, D:D + 1]))
                        b = stats(t - 1, True) if t % CT else None
                        after(m)
                        dve.scalar_tensor_tensor(X[s][:, t, :], ac[:, 0:D], RC[:, t:t + 1], X[s][:, t, :],
                                                 ALU.mult, ALU.add).then_inc(f_free if t < 2 else acc_free, 1)
                        if b:
                            aggregate(t - 1, b)
                        if t % CT == CT - 1:
                            aggregate(t, stats(t, True))

                    def shift(c):
                        cs = slice(CT * c, CT * c + CT)
                        dve.wait_ge(rstd_ready, 4 * U + c + 1)
                        dve.scalar_tensor_tensor(NMR[:, cs], MV[:, cs, 0], -1.0, RS[:, cs], ALU.mult,
                                                 ALU.mult).then_inc(nmr_ready, 1)

                    def ht_lower(c, d):
                        dve.wait_ge(ht_hi, 4 * U + 2 * c + d + 1)
                        dve.scalar_tensor_tensor(HTL[:, d, :], f_bank(h_use(c, d))[:, :], VC[:, GS + d:GS + d + 1],
                                                 HTH[:, d, :], ALU.mult, ALU.subtract).then_inc(f_free, 1)

                    def gelu_lower(c, f):
                        g = FT * c + f
                        dve.wait_ge(g_hi, FF_N * U + g + 1)
                        dve.scalar_tensor_tensor(GL[:, g % GR, :], f_bank(f_use(c, f))[:, :], VC[:, AG:AG + 1],
                                                 GH[:, g % GR, :], ALU.mult, ALU.subtract).then_inc(f_free, 1)

                    def fed(c):
                        dve.wait_ge(r_ready, 2 * U + c + 1)
                        for q in range(CT):
                            t = CT * c + q
                            if q == 0:
                                dve.wait_ge(acc_full, FULL_N * U + NT + c + 1)
                            if q == 2:
                                dve.wait_ge(ff2_done, FF_N * U + FT * (c + 1) + GR)
                            ins = dve.scalar_tensor_tensor(X[s][:, t, :], AC[q // 2][:, (q % 2) * D:(q % 2 + 1) * D],
                                                           VC[:, D2:D2 + 1], X[s][:, t, :], ALU.mult, ALU.add)
                            if q % 2:
                                ins.then_inc(acc_free, 1)

                    def fed_stats(c):
                        dve.wait_ge(acc_free, ACC_N * U + NT + 2 * c + 2)
                        ms = [stats(CT * c + q) for q in range(CT)]
                        for q in range(CT):
                            aggregate(CT * c + q, ms[q])

                    def tail_rows(c):
                        dve.wait_ge(rstd_ready, 4 * U + 3 + c)
                        for t in range(CT * c, CT * c + CT):
                            ins = dve.tensor_scalar(X[s][:, t, :], X[s][:, t, :], MV[:, t, 0:1], RS[:, t:t + 1],
                                                    ALU.subtract, ALU.mult)
                            if t < CT * c + CT - 1 or not last:
                                at = mark(ins)
                            else:
                                ins.then_inc(scored, 1)
                        return [0 if last else at, 0 if last else at]

                    def tail_scores(t, used):
                        if not last:
                            scores(s, t, X[s], used)
                            if t % CT == CT - 1:
                                scores_end(s, t // CT, scored)

                    def new_bias(r):
                        if last:
                            batch_bias(s, 2 * p + s + 2, r)

                    node_parts(o, k)
                    attended(0)
                    attended(1)
                    attended(2)
                    turned(k, 0)
                    attended(3)
                    dve.wait_ge(rows_ready, 2 * k + 1)
                    shift(0)
                    row_max(o, k, 0)
                    attended(4)
                    row_max(o, k, 1)
                    row_max(o, k, 2)
                    attended(5)
                    ht_lower(0, 0)
                    ht_lower(0, 1)
                    row_max(o, k, 3)
                    attended(6)
                    row_max(o, k, 4)
                    row_max(o, k, 5)
                    gelu_lower(0, 0)
                    attended(7)
                    row_max(o, k, 6)
                    gelu_lower(0, 1)
                    row_max(o, k, 7)
                    row_parts(o, k, ab)
                    gelu_lower(0, 2)
                    turned(k, 1)
                    gelu_lower(0, 3)
                    dve.wait_ge(mask_ready, NT * (2 * p + 2) + (NT if last and s else 0))
                    shift(1)
                    larger(o, k, 0)
                    gelu_lower(0, 4)
                    larger(o, k, 1)
                    larger(o, k, 2)
                    larger(o, k, 3)
                    masked(o, k, 0)
                    masked(o, k, 1)
                    x_lower(o, k, VC[:, AXN:AXN + 1] if s else VC[:, AXE:AXE + 1])
                    new_bias(0)
                    gelu_lower(0, 5)
                    new_bias(1)
                    gelu_lower(0, 6)
                    masked(o, k, 2)
                    new_bias(2)
                    gelu_lower(0, 7)
                    ht_lower(1, 0)
                    ht_lower(1, 1)
                    masked(o, k, 3)
                    fed(0)
                    gelu_lower(1, 0)
                    larger(o, k, 4)
                    new_bias(3)
                    gelu_lower(1, 1)
                    larger(o, k, 5)
                    gelu_lower(1, 2)
                    larger(o, k, 6)
                    larger(o, k, 7)
                    masked(o, k, 4)
                    fed_stats(0)
                    new_bias(4)
                    masked(o, k, 5)
                    gelu_lower(1, 3)
                    used = tail_rows(0)
                    new_bias(5)
                    masked(o, k, 6)
                    gelu_lower(1, 4)
                    new_bias(6)
                    masked(o, k, 7)
                    tail_scores(0, used)
                    gelu_lower(1, 5)
                    new_bias(7)
                    tail_scores(1, used)
                    tail_scores(2, used)
                    gelu_lower(1, 6)
                    tail_scores(3, used)
                    gelu_lower(1, 7)
                    fed(1)
                    fed_stats(1)
                    if last:
                        dve.wait_ge(xn_in, 16 * (2 * p + s + 1))
                        batch_stats(2 * p + s + 2, XN)
                    used = tail_rows(1)
                    if last:
                        batch_shift(2 * p + s + 2)
                        dve.wait_ge(scored, 2 * U + 2)
                        xs = X[s][:, CT:NT, :]
                        for b_row, op in ((G2, ALU.mult), (BE2, ALU.add)):
                            link(dve.tensor_tensor(xs, xs, row(b_row, l).unsqueeze(1).to_broadcast([P, CT, D]), op))
                        dve.wait_ge(xo_in, 16 * (2 * (2 * p + s) + 2))
                        dve.tensor_tensor(XO[:, :, :], XO[:, :, :], xs, ALU.add).then_inc(xo_sum, 1)
                        batch_scores(s, 2 * p + s + 2, XN)
                    else:
                        for t in range(CT, NT):
                            tail_scores(t, used)

            steps(dve, body)


_INS = ['x', 'adj', 'L0_gnn_attn_w', 'L0_gnn_attn_b', 'L0_gnn_W1', 'L0_gnn_b1', 'L0_gnn_W2', 'L0_gnn_b2',
        'L0_gnn_g1', 'L0_gnn_beta1', 'L0_gnn_g2', 'L0_gnn_beta2']
_OUTS = [((8, 1024, 256), 'float32')]


def kernel(**inputs):
    import numpy as _np
    import concourse.bacc as _bacc
    from concourse import mybir as _mybir
    from concourse.bass_utils import run_bass_kernel_spmd as _run

    nc = _bacc.Bacc("TRN2", target_bir_lowering=False, num_devices=1)
    arrays, args = {}, []
    for name in _INS:
        a = _np.ascontiguousarray(inputs[name])
        arrays[f"in_{name}_dram"] = a
        args.append(nc.dram_tensor(f"in_{name}_dram", a.shape, _mybir.dt.from_np(a.dtype), kind="ExternalInput").ap())
    for i, (shape, dtype) in enumerate(_OUTS):
        dt = _mybir.dt.from_np(_np.dtype(dtype))
        args.append(nc.dram_tensor(f"out_{i}_dram", shape, dt, kind="ExternalOutput").ap())
    gnn_kernel(nc, *args)
    r = _run(nc, [arrays], core_ids=[0])
    got = tuple(r.results[0][f"out_{i}_dram"] for i in range(len(_OUTS)))
    return got[0]
```
